# Optimizing a Trainium2 kernel written in Bass

```python
import numpy as np
import jax
import jax.numpy as jnp

def _softmax(x, axis=-1):
    return jax.nn.softmax(x, axis=axis)

def _gelu(x):
    return jax.nn.gelu(x, approximate=True)

def _silu(x):
    return jax.nn.silu(x)

def _sigmoid(x):
    return jax.nn.sigmoid(x)

def _layernorm(x, axis=-1, eps=1e-05):
    m = jnp.mean(x, axis=axis, keepdims=True)
    v = jnp.var(x, axis=axis, keepdims=True)
    return (x - m) / jnp.sqrt(v + eps)

def _scatter_add(tgt, idx, src, axis=0):
    return tgt.at[idx].add(src)

def _segment_sum(src, seg, n):
    return jax.ops.segment_sum(src, seg, n)
kernel_name = 'mk_adaln_ffn_d1_seqx_r2_032373'

def setup_inputs(seed: int=0):
    np.random.seed(seed)
    _w = jnp.asarray

    def _rec_inputs():
        import jax
        import jax.numpy as jnp
        _rk = jax.random.key(seed)
        x = -0.000125 + 0.9999 * jax.random.normal(jax.random.fold_in(_rk, 1), (2, 2048, 512), jnp.float32)
        _lenS = 2048 - jax.random.randint(jax.random.fold_in(_rk, 7), (2,), 0, max(1, 2048 // 4) + 1, jnp.int32)
        _lenS2 = 2048 - jax.random.randint(jax.random.fold_in(_rk, 8), (2,), 0, max(1, 2048 // 4) + 1, jnp.int32)
        cond_1024 = jax.random.uniform(jax.random.fold_in(_rk, 11), (2, 512), jnp.float32, 0.0, 0.999927)
        return (x, cond_1024)
    x, cond_1024 = _rec_inputs()

    def _L0_cond_setup():
        import jax, jax.numpy as jnp
        import numpy as np
        DT = 0.001
        key = jax.random.key(seed)
        k1, k2 = jax.random.split(key)
        inputs = jax.random.normal(k1, (16, 1024, 512), dtype=jnp.float32)
        initial_state = jax.random.uniform(k2, (16, 512), dtype=jnp.float32)
        return {'inputs': inputs, 'initial_state': initial_state}
    _L0_cond_all = _L0_cond_setup()
    _L0_cond_in = {k: v for k, v in _L0_cond_all.items() if k in ()}
    del _L0_cond_all

    def _L0_ffn_setup():
        import jax, jax.numpy as jnp
        import numpy as np
        B, S, D = (4, 1024, 512)
        N_EXPERTS, EXPERT_SIZE = (16, 128)
        WIDTH = N_EXPERTS * EXPERT_SIZE
        key = jax.random.key(seed)
        k_x, k_w1, k_w2, k_g = jax.random.split(key, 4)
        x = jax.random.normal(k_x, (B, S, D), dtype=jnp.float32)
        w1 = jax.random.normal(k_w1, (D, WIDTH), dtype=jnp.float32) / np.sqrt(D).astype(np.float32)
        b1 = jnp.zeros((WIDTH,), dtype=jnp.float32)
        w2 = jax.random.normal(k_w2, (WIDTH, D), dtype=jnp.float32) / np.sqrt(WIDTH).astype(np.float32)
        b2 = jnp.zeros((D,), dtype=jnp.float32)
        return {'x': x, 'w1': w1, 'b1': b1, 'w2': w2, 'b2': b2}
    _L0_ffn_all = _L0_ffn_setup()
    _L0_ffn_in = {k: v for k, v in _L0_ffn_all.items() if k in ('w1', 'b1', 'w2', 'b2')}
    del _L0_ffn_all
    return {'x': x, 'cond_1024': cond_1024, 'L0_ffn_w1': _L0_ffn_in['w1'], 'L0_ffn_b1': _L0_ffn_in['b1'], 'L0_ffn_w2': _L0_ffn_in['w2'], 'L0_ffn_b2': _L0_ffn_in['b2']}

def reference(x, cond_1024, L0_ffn_w1, L0_ffn_b1, L0_ffn_w2, L0_ffn_b2):
    import jax
    import jax.numpy as jnp

    def _L0_cond_ref(inputs, initial_state):
        import jax, jax.numpy as jnp
        import numpy as np
        DT = 0.001
        rates = jax.nn.relu(inputs) * DT
        c = initial_state[:, None, :] + jnp.cumsum(rates, axis=1)
        fl = jnp.floor(c)
        prev = jnp.concatenate([jnp.floor(initial_state)[:, None, :], fl[:, :-1, :]], axis=1)
        spikes = fl - prev
        return spikes / DT

    def _L0_ffn_ref(x, w1, b1, w2, b2):
        import jax, jax.numpy as jnp
        import numpy as np
        B, S, D = (4, 1024, 512)
        N_EXPERTS, EXPERT_SIZE = (16, 128)
        WIDTH = N_EXPERTS * EXPERT_SIZE
        h = jax.nn.relu(jnp.einsum('bsd,dw->bsw', x, w1) + b1)
        return jnp.einsum('bsw,wd->bsd', h, w2) + b2
    x = x + _L0_ffn_ref(_L0_cond_ref(x, cond_1024), L0_ffn_w1, L0_ffn_b1, L0_ffn_w2, L0_ffn_b2)
    return x

_drawn_inputs = setup_inputs


def setup_inputs(seed=0):
    import zlib

    import numpy as np

    out = dict(_drawn_inputs(seed))
    spreads = {'L0_ffn_b1': (0.0, 0.8), 'L0_ffn_b2': (0.0, 0.8)}
    factors = {}
    for name, (base, spread) in spreads.items():
        noise = np.random.default_rng([zlib.crc32(name.encode()), seed]).standard_normal(out[name].shape)
        drawn = base * np.exp(spread * noise) if base else spread * noise
        out[name] = jnp.asarray(drawn.astype(out[name].dtype))
    for name, factor in factors.items():
        out[name] = (out[name] * factor).astype(out[name].dtype)
    return out
```

```python
from contextlib import ExitStack

import numpy as np
import concourse.bass as bass
from concourse import mybir

ALU = mybir.AluOpType
ACT = mybir.ActivationFunctionType
AX = mybir.AxisListType
F32 = mybir.dt.float32
BF16 = mybir.dt.bfloat16
I32 = mybir.dt.int32

P = 128
DT = 0.001
PER_DT = float(np.float32(1.0 / float(np.float32(DT))))
ROUND = float(2 ** 23)


def spike_ffn(nc, x, cond, w1, b1, w2, b2, spikes_dram, out):
    B, S, D = x.shape
    F = w1.shape[1]
    BLK = S // P
    DC = D // P
    FC = F // P
    SUP = P // BLK
    NT = S // P
    ROWS = B * S
    XQ = 4
    TQ = BLK // XQ
    assert BLK == 16 and SUP == 8 and D == 512

    x_blk = x.rearrange("b (p t) d -> b p t d", t=BLK)
    out_blk = out.rearrange("b (p t) d -> b p t d", t=BLK)
    spk_blk = [s.rearrange("(p t) d -> p t d", t=BLK) for s in spikes_dram]
    x_rows = x.rearrange("b s d -> (b s) d")
    out_rows = out.rearrange("b s d -> (b s) d")

    with ExitStack() as ctx:
        def sb(name, shape, dt=F32):
            return ctx.enter_context(nc.sbuf_tensor(name, shape, dt))

        def sem(name):
            return ctx.enter_context(nc.semaphore(name))

        def psum(name):
            return ctx.enter_context(nc.psum_tensor(name, [P, 512], F32))

        x_keep = sb("x_keep", [P, BLK, D])
        acc = [sb(f"acc{b}", [P, BLK, D]) for b in range(B)]
        w1_sb = sb("w1_sb", [P, DC, F])
        w2_sb = sb("w2_sb", [P, FC, D])
        b1_rows = sb("b1_rows", [FC, P])
        b1_col = sb("b1_col", [P, FC])
        relu_b1 = sb("relu_b1", [P, FC])
        b2_all = sb("b2_all", [P, D])
        idle_row = sb("idle_row", [P, D])
        init_all = sb("init_all", [P, B, D])
        ident = sb("ident", [P, P])
        upper = sb("upper", [P, P])
        ones = sb("ones", [P, P])
        block_keep = sb("block_keep", [P, DC * P])
        group_keep = sb("group_keep", [P, DC * SUP])
        level1 = sb("level1", [P, DC * P])
        level2 = sb("level2", [P, DC * SUP])
        level2_before = sb("level2_before", [P, DC, SUP + 1])
        block_sum = sb("block_sum", [P, DC, P + 1])
        scratch = sb("scratch", [P, 2, D])
        rounded, above = scratch[:, 0, :], scratch[:, 1, :]
        last_floor = level1
        first_prev = sb("first_prev", [P, D])
        spike_sum = sb("spike_sum", [P, B, BLK])
        active = sb("active", [P, BLK])
        active_run = sb("active_run", [P, BLK])
        rank_f = sb("rank_f", [P, BLK])
        rank_i = sb("rank_i", [P, BLK], I32)
        rank_tile = sb("rank_tile", [P, BLK], I32)
        rank_slot = sb("rank_slot", [P, BLK], I32)
        slot_b = sb("slot_b", [P, BLK], BF16)
        tile_b = sb("tile_b", [P, BLK], BF16)
        active_b = sb("active_b", [P, BLK], BF16)
        iota_i = sb("iota_i", [P, P], I32)
        iota_b = sb("iota_b", [P, P], BF16)
        part_i = sb("part_i", [P, 1], I32)
        part_f = sb("part_f", [P, 1])
        slot_hot = scratch[:, :, :].rearrange("p a d -> p (a d)").bitcast(BF16).rearrange("p (t k) -> p t k", k=P)
        tile_hot = sb("tile_hot", [P, BLK, 3, NT], BF16)
        found = sb("found", [P, 3, NT])
        row_id = sb("row_id", [P, NT])
        missing = sb("missing", [P, NT])
        gather_at = [sb(f"gather_at{b}", [P, NT + 1, 2], I32) for b in range(B)]
        scatter_at = [sb(f"scatter_at{b}", [P, NT + 1], I32) for b in range(B)]
        tiles_f = sb("tiles_f", [P, 1])
        tiles_i = [sb(f"tiles_i{b}", [P, 1], I32) for b in range(B)]
        gather_col = [sb(f"gather_col{i}", [P, 2], I32) for i in range(2)]
        scatter_col = sb("scatter_col", [P, 1], I32)
        spk_rows = [sb(f"spk_rows{i}", [P, D]) for i in range(2)]
        x_got = [sb(f"x_got{i}", [P, D]) for i in range(2)]
        spk_t = sb("spk_t", [P, DC, P])
        hidden = sb("hidden", [P, FC, P])
        relu_b1_wide = hidden
        ffn = sb("ffn", [P, D])

        ps_turn = psum("ps_turn")
        ps_before = psum("ps_before")
        ps_small = psum("ps_small")
        ps_idle = psum("ps_idle")
        ps_hidden = [psum("ps_hidden0"), psum("ps_hidden1")]
        ps_spk = psum("ps_spk")
        ps_out = psum("ps_out")

        x_in = [[sem(f"x_in{b}_{q}") for q in range(XQ)] for b in range(B)]
        init_in = sem("init_in")
        w1_in = sem("w1_in")
        w2_in = sem("w2_in")
        b1_in = sem("b1_in")
        b2_in = sem("b2_in")
        const_ready = sem("const_ready")
        pool_step = sem("pool_step")
        rates_ready = sem("rates_ready")
        sums_ready = [sem(f"sums_ready{b}") for b in range(B)]
        totals_turned = sem("totals_turned")
        before_ready = sem("before_ready")
        before_turned = sem("before_turned")
        b1_turned = sem("b1_turned")
        b1_wide = sem("b1_wide")
        idle_summed = sem("idle_summed")
        idle_ready = sem("idle_ready")
        idle_added = sem("idle_added")
        idle_stored = [sem(f"idle_stored{b}") for b in range(B)]
        x_again = sem("x_again")
        dve_step = sem("dve_step")
        edge_ready = sem("edge_ready")
        edge_in = [sem(f"edge_in{b}") for b in range(B)]
        spikes_ready = [sem(f"spikes_ready{b}") for b in range(B)]
        spikes_stored = [sem(f"spikes_stored{b}") for b in range(B)]
        row_counts = sem("row_counts")
        row_offsets = sem("row_offsets")
        hots_ready = sem("hots_ready")
        found_ready = sem("found_ready")
        list_ready = sem("list_ready")
        spk_got = [[sem(f"spk_got{b}_{i}") for i in range(2)] for b in range(B)]
        xrow_got = [[sem(f"xrow_got{b}_{i}") for i in range(2)] for b in range(B)]
        spk_turned = [sem(f"spk_turned{b}") for b in range(B)]
        spk_copied = [sem(f"spk_copied{b}") for b in range(B)]
        hidden_summed = [sem(f"hidden_summed{b}") for b in range(B)]
        hidden_ready = [sem(f"hidden_ready{b}") for b in range(B)]
        out_summed = [sem(f"out_summed{b}") for b in range(B)]
        ffn_ready = [sem(f"ffn_ready{b}") for b in range(B)]
        col_copied = sem("col_copied")
        row_added = sem("row_added")
        ffn_used = [sem(f"ffn_used{b}") for b in range(B)]
        scattered = [sem(f"scattered{b}") for b in range(B)]

        block = ctx.enter_context(nc.Block())

        @block.sync
        def _(sp):
            def piece(b, q):
                return x_blk[b, :, q * TQ:(q + 1) * TQ, :]

            for q in range(XQ):
                sp.dma_start(x_keep[:, q * TQ:(q + 1) * TQ, :], piece(0, q)).then_inc(x_in[0][q], 16)
            sp.dma_start(init_all[:, :, :], cond.rearrange("(o b) d -> o b d", o=1).to_broadcast([P, B, D])).then_inc(init_in, 16)
            sp.dma_start(b1_rows[:, :], b1.rearrange("(c p) -> c p", p=P)).then_inc(b1_in, 16)
            sp.dma_start(b2_all[:, :], b2.rearrange("(o d) -> o d", o=1).to_broadcast([P, D])).then_inc(b2_in, 16)
            sp.dma_start(w2_sb[:, :, :], w2.rearrange("(c p) d -> p c d", p=P)).then_inc(w2_in, 16)
            for q in range(XQ):
                sp.dma_start(acc[1][:, q * TQ:(q + 1) * TQ, :], piece(1, q)).then_inc(x_in[1][q], 16)
            sp.dma_start(w1_sb[:, :, :], w1.rearrange("(c p) f -> p c f", p=P)).then_inc(w1_in, 16)
            for b in range(B):
                if b == 1:
                    for q in range(XQ):
                        sp.wait_ge(idle_added, q + 1)
                        sp.dma_start(out_blk[0, :, q * TQ:(q + 1) * TQ, :],
                                     x_keep[:, q * TQ:(q + 1) * TQ, :]).then_inc(idle_stored[0], 16)
                sp.wait_ge(edge_ready, b + 1)
                sp.dma_start(first_prev[1:P, :], last_floor[0:P - 1, :]).then_inc(edge_in[b], 16)
                for q in range(XQ):
                    sp.wait_ge(spikes_ready[b], q + 1)
                    r = XQ - 1 - q
                    sp.dma_start(spk_blk[b][:, r * TQ:(r + 1) * TQ, :],
                                 acc[b][:, r * TQ:(r + 1) * TQ, :]).then_inc(spikes_stored[b], 16)
                if b == 0:
                    pass
                if b == 1:
                    sp.wait_ge(idle_stored[0], 16 * XQ)
                    sp.dma_start(x_keep[:, :, :], x_blk[1]).then_inc(x_again, 16)
                    sp.wait_ge(idle_added, XQ + 1)
                    sp.dma_start(out_blk[1], x_keep[:, :, :]).then_inc(idle_stored[1], 16)
            sp.wait_ge(idle_stored[1], 16)

        @block.gpsimd
        def _(pool):
            steps = [0]

            def chain(ins):
                steps[0] += 1
                ins.then_inc(pool_step, 1)
                pool.wait_ge(pool_step, steps[0])

            chain(pool.memset(ident[:, :], 0.0))
            chain(pool.memset(ones[:, :], 1.0))
            pool.affine_select(out=ident[:, :], in_=ident[:, :], compare_op=ALU.not_equal, fill=1.0, base=0,
                               pattern=[[-1, P]], channel_multiplier=1).then_inc(const_ready, 1)
            pool.affine_select(out=upper[:, :], in_=ones[:, :], compare_op=ALU.is_gt, fill=0.0, base=0,
                               pattern=[[1, P]], channel_multiplier=-1).then_inc(const_ready, 1)
            pool.iota(iota_i[:, :], pattern=[[1, P]], base=0, channel_multiplier=0).then_inc(const_ready, 1)
            pool.iota(part_i[:, :], pattern=[[1, 1]], base=0, channel_multiplier=1).then_inc(const_ready, 1)

            for b in range(B):
                pool.sem_inc(ffn_used[b], 1)

            for t in range(1, BLK):
                pool.wait_ge(rates_ready, XQ + t // TQ + 1)
                chain(pool.tensor_tensor(acc[1][:, t, :], acc[1][:, t, :], acc[1][:, t - 1, :], ALU.add))
            pool.memset(level2_before[:, :, 0:1], 0.0).then_inc(sums_ready[1], 1)

            pool.wait_ge(idle_ready, 1)
            for q in range(XQ):
                pool.wait_ge(x_in[0][q], 16)
                pool.wait_ge(rates_ready, q + 1)
                for t in range(q * TQ, (q + 1) * TQ):
                    last = pool.tensor_tensor(x_keep[:, t, :], x_keep[:, t, :], idle_row[:, :], ALU.add)
                    if t < (q + 1) * TQ - 1:
                        chain(last)
                last.then_inc(idle_added, 1)

            for b in range(B):
                pool.wait_ge(list_ready, b + 1)
                tiles = pool.value_load(tiles_i[b][0:1, 0:1], min_val=0, max_val=NT)
                pool.wait_ge(spikes_stored[b], 16 * XQ)
                last_row = pool.to_reg(ROWS - 1)

                def gather(tile, side):
                    pool.tensor_copy(gather_col[side][:, :], gather_at[b][:, bass.ds(tile, 1), :].rearrange("p o a -> p (o a)")).then_inc(col_copied, 1)
                    pool.wait_ge(col_copied, 1)
                    pool.sem_clear(col_copied)
                    in_batch = bass.IndirectOffsetOnAxis(ap=gather_col[side][:, 0:1], axis=0)
                    in_all = bass.IndirectOffsetOnAxis(ap=gather_col[side][:, 1:2], axis=0)
                    pool.indirect_dma_start(out=spk_rows[side][:, :], out_offset=None,
                                            in_=spikes_dram[b], in_offset=in_batch).then_inc(spk_got[b][side], 16)
                    pool.indirect_dma_start(out=x_got[side][:, :], out_offset=None,
                                            in_=x_rows, in_offset=in_all).then_inc(xrow_got[b][side], 16)

                gather(0, 0)
                pool.wait_ge(idle_stored[b], 16 * (XQ if b == 0 else 1))
                pool.wait_ge(spk_got[b][0], 16)
                pool.wait_ge(xrow_got[b][0], 16)
                with pool.Fori(0, NT // 2) as pair:
                    for side in range(2):
                        with pool.If(pair * 2 + side < tiles):
                            pool.wait_ge(spk_turned[b], pair * 2 + side + 1)
                            pool.tensor_tensor(x_got[side][:, :], x_got[side][:, :], b2_all[:, :], ALU.add)
                            gather(pair * 2 + side + 1, 1 - side)
                            pool.tensor_copy(scatter_col[:, :], scatter_at[b][:, bass.ds(pair * 2 + side, 1)]).then_inc(row_added, 1)
                            pool.wait_ge(ffn_ready[b], pair * 2 + side + 1)
                            pool.tensor_tensor(x_got[side][:, :], ffn[:, :], x_got[side][:, :], ALU.add).then_inc(row_added, 1)
                            pool.wait_ge(row_added, 2)
                            pool.sem_clear(row_added)
                            pool.sem_inc(ffn_used[b], 1)
                            pool.indirect_dma_start(
                                out=out_rows, out_offset=bass.IndirectOffsetOnAxis(ap=scatter_col[:, :], axis=0),
                                in_=x_got[side][:, :], in_offset=None, bounds_check=last_row,
                                oob_is_err=False).then_inc(scattered[b], 16)
                            pool.wait_ge(scattered[b], pair * 32 + side * 16 + 16)
                            if side == 0:
                                pool.wait_ge(spk_got[b][1], pair * 16 + 16)
                                pool.wait_ge(xrow_got[b][1], pair * 16 + 16)
                            else:
                                pool.wait_ge(spk_got[b][0], pair * 16 + 32)
                                pool.wait_ge(xrow_got[b][0], pair * 16 + 32)

        @block.scalar
        def _(act):
            for b in range(B):
                src = x_keep if b == 0 else acc[1]
                for q in range(XQ):
                    act.wait_ge(x_in[b][q], 16)
                    act.activation(acc[b][:, q * TQ:(q + 1) * TQ, :], src[:, q * TQ:(q + 1) * TQ, :],
                                   ACT.Relu, scale=DT).then_inc(rates_ready, 1)
                if b == 0:
                    act.wait_ge(b1_turned, 1)
                    act.activation(b1_col[:, :], ps_small[:, 0:FC], ACT.Copy).then_inc(b1_wide, 1)
                    act.wait_ge(b1_wide, 1)
                    act.activation(relu_b1[:, :], b1_col[:, :], ACT.Relu).then_inc(b1_wide, 1)
                    act.wait_ge(b1_wide, 2)
                    act.activation(relu_b1_wide[:, :, :], relu_b1[:, :].rearrange("p (c o) -> p c o", o=1).to_broadcast([P, FC, P]),
                                   ACT.Copy).then_inc(b1_wide, 1)

            for b in range(B):
                act.wait_ge(list_ready, b + 1)
                tiles = act.value_load(tiles_i[b][0:1, 0:1], min_val=0, max_val=NT)
                with act.Fori(0, NT) as t:
                    with act.If(t < tiles):
                        act.wait_ge(spk_turned[b], t + 1)
                        act.activation(spk_t[:, :, :], ps_spk[:, :], ACT.Copy).then_inc(spk_copied[b], 1)
                        for m in range(FC):
                            act.wait_ge(hidden_summed[b], t * FC + m + 1)
                            act.activation(hidden[:, m, :], ps_hidden[m % 2][:, 0:P], ACT.Relu,
                                           bias=b1_col[:, m:m + 1], scale=PER_DT).then_inc(hidden_ready[b], 1)
                        act.wait_ge(out_summed[b], t + 1)
                        act.wait_ge(ffn_used[b], t + 1)
                        act.activation(ffn[:, :], ps_out[:, :], ACT.Copy).then_inc(ffn_ready[b], 1)

        @block.vector
        def _(dve):
            steps = [0]

            def chain(ins):
                steps[0] += 1
                ins.then_inc(dve_step, 1)
                dve.wait_ge(dve_step, steps[0])

            dve.memset(block_keep[:, :], 1.0)
            chain(dve.memset(group_keep[:, :], 1.0))
            dve.memset(block_keep[:, :].rearrange("p (g k) -> p g k", k=BLK)[:, :, 0:1], 0.0)
            dve.memset(group_keep[:, :].rearrange("p (c g) -> p c g", g=SUP)[:, :, 0:1], 0.0)
            chain(dve.memset(block_sum[:, :, 0:1], 0.0))
            for b in range(B):
                dve.memset(gather_at[b][:, :, :], 0)
                chain(dve.memset(scatter_at[b][:, :], 0))

            dve.wait_ge(init_in, 16)

            for t in range(1, BLK):
                dve.wait_ge(rates_ready, t // TQ + 1)
                last = dve.tensor_tensor(acc[0][:, t, :], acc[0][:, t, :], acc[0][:, t - 1, :], ALU.add)
                if t < BLK - 1:
                    chain(last)
            last.then_inc(sums_ready[0], 1)

            def block_prefix(b):
                dve.wait_ge(totals_turned, b + 1)
                chain(dve.tensor_tensor_scan(level1[:, :], block_keep[:, :], ps_turn[:, :], 0.0, ALU.mult, ALU.add))
                groups = level1[:, :].rearrange("p (c k) -> p c k", k=BLK)
                chain(dve.tensor_tensor_scan(level2[:, :], group_keep[:, :], groups[:, :, BLK - 1], 0.0,
                                             ALU.mult, ALU.add))
                dve.wait_ge(sums_ready[1], 1)
                chain(dve.tensor_copy(level2_before[:, :, 1:SUP + 1], level2[:, :].rearrange("p (c g) -> p c g", g=SUP)))
                if b > 0:
                    dve.wait_ge(before_turned, b)
                dve.tensor_tensor(
                    block_sum[:, :, 1:P + 1].rearrange("p c (g k) -> p c g k", k=BLK),
                    level1[:, :].rearrange("p (c g k) -> p c g k", g=SUP, k=BLK),
                    level2_before[:, :, 0:SUP].rearrange("p c (g o) -> p c g o", o=1).to_broadcast([P, DC, SUP, BLK]),
                    ALU.add).then_inc(before_ready, 1)

            block_prefix(0)
            dve.wait_ge(idle_summed, 1)
            dve.wait_ge(b2_in, 16)
            dve.tensor_tensor(idle_row[:, :], ps_idle[:, :], b2_all[:, :], ALU.add).then_inc(idle_ready, 1)

            for b in range(B):
                start = init_all[0:1, b, :]
                chain(dve.tensor_scalar(rounded[0:1, :], start, ROUND, -ROUND, ALU.add, ALU.add))
                chain(dve.tensor_tensor(above[0:1, :], rounded[0:1, :], start, ALU.is_gt))
                chain(dve.tensor_tensor(first_prev[0:1, :], rounded[0:1, :], above[0:1, :], ALU.subtract))
                dve.wait_ge(before_turned, b + 1)
                for t in range(BLK - 1, -1, -1):
                    row = acc[b][:, t, :]
                    chain(dve.tensor_tensor(row, row, ps_before[:, :], ALU.add))
                    chain(dve.tensor_tensor(row, row, init_all[:, b, :], ALU.add))
                    chain(dve.tensor_scalar(rounded, row, ROUND, -ROUND, ALU.add, ALU.add))
                    chain(dve.tensor_tensor(above, rounded, row, ALU.is_gt))
                    if t == BLK - 1:
                        dve.tensor_tensor(last_floor[:, :], rounded, above, ALU.subtract).then_inc(edge_ready, 1)
                        dve.wait_ge(edge_ready, b + 1)
                        chain(dve.tensor_copy(row, last_floor[:, :]))
                    else:
                        chain(dve.tensor_tensor(row, rounded, above, ALU.subtract))
                        nxt = acc[b][:, t + 1, :]
                        ins = dve.tensor_tensor(nxt, nxt, row, ALU.subtract)
                        if (t + 1) % TQ == 0:
                            ins.then_inc(spikes_ready[b], 1)
                            dve.wait_ge(spikes_ready[b], (BLK - t - 1) // TQ)
                        else:
                            chain(ins)
                dve.wait_ge(edge_in[b], 16)
                dve.tensor_tensor(acc[b][:, 0, :], acc[b][:, 0, :], first_prev[:, :], ALU.subtract).then_inc(spikes_ready[b], 1)
                dve.wait_ge(spikes_ready[b], XQ)
                chain(dve.tensor_reduce(spike_sum[:, b, :], acc[b][:, :, :], AX.X, ALU.max, apply_absolute_value=True))

                if b == 0:
                    block_prefix(1)
                    dve.wait_ge(before_turned, 2)
                chain(dve.tensor_scalar(active[:, :], spike_sum[:, b, :], 0.0, None, ALU.is_gt))
                dve.tensor_copy(active_b[:, :], active[:, :])
                dve.tensor_tensor_scan(active_run[:, :], ones[:, 0:BLK], active[:, :], 0.0, ALU.mult,
                                       ALU.add).then_inc(row_counts, 1)
                if b == 0:
                    dve.wait_ge(const_ready, 4)
                    dve.tensor_copy(iota_b[:, :], iota_i[:, :])
                    chain(dve.tensor_copy(part_f[:, :], part_i[:, :]))
                dve.wait_ge(row_offsets, b + 1)
                chain(dve.scalar_tensor_tensor(out=rank_f[:, :], in0=active_run[:, :], scalar=ps_small[:, 0:1],
                                               in1=active[:, :], op0=ALU.add, op1=ALU.subtract))
                chain(dve.tensor_scalar(tiles_f[:, :], ps_small[:, 1:2], float(P - 1), None, ALU.add))
                dve.tensor_copy(tiles_i[b][:, :], tiles_f[:, :])
                chain(dve.tensor_copy(rank_i[:, :], rank_f[:, :]))
                dve.tensor_scalar(tiles_i[b][:, :], tiles_i[b][:, :], 7, None, ALU.arith_shift_right)
                dve.tensor_scalar(rank_tile[:, :], rank_i[:, :], 7, None, ALU.arith_shift_right)
                chain(dve.tensor_scalar(rank_slot[:, :], rank_i[:, :], P - 1, None, ALU.bitwise_and))
                dve.tensor_copy(tile_b[:, :], rank_tile[:, :])
                chain(dve.tensor_copy(slot_b[:, :], rank_slot[:, :]))

                def over(ap, n):
                    return ap.rearrange("p (t o) -> p t o", o=1).to_broadcast([P, BLK, n])

                def along(ap, n):
                    return ap.rearrange("p (o k) -> p o k", o=1).to_broadcast([P, BLK, n])

                dve.tensor_tensor(slot_hot, over(slot_b[:, :], P), along(iota_b[:, :], P), ALU.is_equal)
                chain(dve.tensor_tensor(tile_hot[:, :, 0, :], over(tile_b[:, :], NT), along(iota_b[:, 0:NT], NT), ALU.is_equal))
                chain(dve.tensor_tensor(tile_hot[:, :, 0, :], tile_hot[:, :, 0, :], over(active_b[:, :], NT), ALU.mult))
                dve.tensor_scalar(tile_hot[:, :, 1, :], tile_hot[:, :, 0, :], part_f[:, 0:1], None, ALU.mult).then_inc(hots_ready, 1)
                dve.tensor_tensor(tile_hot[:, :, 2, :], tile_hot[:, :, 0, :], over(iota_b[:, 0:BLK], NT), ALU.mult).then_inc(hots_ready, 1)
                dve.wait_ge(found_ready, b + 1)
                chain(dve.tensor_copy(found[:, :, :], ps_small[:, 64:64 + 3 * NT].rearrange("p (a k) -> p a k", k=NT)))
                dve.tensor_scalar(missing[:, :], found[:, 0, :], -float(ROWS), float(ROWS + b * S), ALU.mult, ALU.add)
                chain(dve.scalar_tensor_tensor(out=row_id[:, :], in0=found[:, 1, :], scalar=float(BLK),
                                               in1=found[:, 2, :], op0=ALU.mult, op1=ALU.add))
                chain(dve.tensor_tensor(missing[:, :], missing[:, :], row_id[:, :], ALU.add))
                chain(dve.tensor_copy(gather_at[b][:, 0:NT, 0], row_id[:, :]))
                chain(dve.tensor_scalar(gather_at[b][:, 0:NT, 1], row_id[:, :], float(b * S), None, ALU.add))
                dve.tensor_copy(scatter_at[b][:, 0:NT], missing[:, :]).then_inc(list_ready, 1)

            dve.wait_ge(x_again, 16)
            dve.wait_ge(idle_ready, 1)
            dve.tensor_tensor(x_keep[:, :, :], x_keep[:, :, :],
                              idle_row[:, :].rearrange("p (o d) -> p o d", o=1).to_broadcast([P, BLK, D]),
                              ALU.add).then_inc(idle_added, 1)

        @block.tensor
        def _(pe):
            pe.wait_ge(const_ready, 2)

            def turn_totals(b):
                pe.wait_ge(sums_ready[b], 1)
                if b > 0:
                    pe.wait_ge(before_ready, b)
                for c in range(DC):
                    last = pe.transpose(ps_turn[:, c * P:(c + 1) * P], acc[b][:, BLK - 1, c * P:(c + 1) * P], ident[:, :])
                last.then_inc(totals_turned, 1)

            def turn_before(b):
                pe.wait_ge(before_ready, b + 1)
                for c in range(DC):
                    last = pe.transpose(ps_before[:, c * P:(c + 1) * P], block_sum[:, c, 0:P], ident[:, :])
                last.then_inc(before_turned, 1)

            pe.wait_ge(b1_in, 16)
            pe.transpose(ps_small[:, 0:FC], b1_rows[:, :], ident[0:FC, 0:FC]).then_inc(b1_turned, 1)
            turn_totals(0)
            turn_before(0)
            pe.wait_ge(b1_wide, 3)
            pe.wait_ge(w2_in, 16)
            for m in range(FC):
                last = pe.matmul(ps_idle[:, :], relu_b1_wide[:, m, :], w2_sb[:, m, :], start=(m == 0), stop=(m == FC - 1))
            last.then_inc(idle_summed, 1)
            turn_totals(1)

            for b in range(B):
                if b == 0:
                    pe.wait_ge(spikes_ready[0], XQ)
                    turn_before(1)
                pe.wait_ge(row_counts, b + 1)
                pe.matmul(ps_small[:, 0:1], upper[:, :], active_run[:, BLK - 1:BLK], start=True, stop=True)
                pe.matmul(ps_small[:, 1:2], ones[:, :], active_run[:, BLK - 1:BLK], start=True, stop=True).then_inc(row_offsets, 1)
                pe.wait_ge(hots_ready, 2 * b + 2)
                for t in range(BLK):
                    last = pe.matmul(ps_small[:, 64:64 + 3 * NT], slot_hot[:, t, :],
                                     tile_hot[:, t, :, :].rearrange("p a k -> p (a k)"), start=(t == 0), stop=(t == BLK - 1))
                last.then_inc(found_ready, 1)
                pe.wait_ge(list_ready, b + 1)
                tiles = pe.value_load(tiles_i[b][0:1, 0:1], min_val=0, max_val=NT)
                if b == 0:
                    pe.wait_ge(w1_in, 16)

                with pe.Fori(0, NT // 2) as pair:
                    for side in range(2):
                        with pe.If(pair * 2 + side < tiles):
                            pe.wait_ge(spk_got[b][side], pair * 16 + 16)
                            for c in range(DC):
                                last = pe.transpose(ps_spk[:, c * P:(c + 1) * P], spk_rows[side][:, c * P:(c + 1) * P], ident[:, :])
                            last.then_inc(spk_turned[b], 1)
                            pe.wait_ge(spk_copied[b], pair * 2 + side + 1)
                            for m in range(FC):
                                if m >= 2:
                                    pe.wait_ge(hidden_ready[b], pair * 2 * FC + side * FC + m - 1)
                                for c in range(DC):
                                    last = pe.matmul(ps_hidden[m % 2][:, 0:P], w1_sb[:, c, m * P:(m + 1) * P],
                                                     spk_t[:, c, :], start=(c == 0), stop=(c == DC - 1))
                                last.then_inc(hidden_summed[b], 1)
                            for m in range(FC):
                                pe.wait_ge(hidden_ready[b], pair * 2 * FC + side * FC + m + 1)
                                last = pe.matmul(ps_out[:, :], hidden[:, m, :], w2_sb[:, m, :],
                                                 start=(m == 0), stop=(m == FC - 1))
                            last.then_inc(out_summed[b], 1)


def kernel(**inputs):
    import concourse.bacc as bacc
    from concourse.bass_utils import run_bass_kernel_spmd

    nc = bacc.Bacc("TRN2", target_bir_lowering=False, num_devices=1)
    arrays, args = {}, []
    for name in ["x", "cond_1024", "L0_ffn_w1", "L0_ffn_b1", "L0_ffn_w2", "L0_ffn_b2"]:
        a = np.ascontiguousarray(inputs[name])
        arrays[f"in_{name}"] = a
        args.append(nc.dram_tensor(f"in_{name}", a.shape, mybir.dt.from_np(a.dtype), kind="ExternalInput").ap())
    shape = inputs["x"].shape
    spikes = [nc.dram_tensor(f"spikes{b}", shape[1:], F32, kind="Internal").ap() for b in range(shape[0])]
    out = nc.dram_tensor("out", shape, F32, kind="ExternalOutput").ap()
    spike_ffn(nc, *args, spikes, out)
    r = run_bass_kernel_spmd(nc, [arrays], core_ids=[0])
    return r.results[0]["out"]
```

```python
from contextlib import ExitStack

import numpy as np
import concourse.bass as bass
from concourse import mybir

ALU = mybir.AluOpType
ACT = mybir.ActivationFunctionType
F32 = mybir.dt.float32
BF16 = mybir.dt.bfloat16
I32 = mybir.dt.int32

P = 128
DT = 0.001
PER_DT = float(np.float32(1.0 / float(np.float32(DT))))


def spike_ffn(nc, x, cond, w1, b1, w2, b2, spikes_dram, table_dram, out):
    B, S, D = x.shape
    F = w1.shape[1]
    BLK = S // P
    DC = D // P
    FC = F // P
    SUP = P // BLK
    TOK = B * BLK
    NT = B * S // P + 1
    ROWS = B * S
    XQ = 4
    TQ = BLK // XQ
    RING = 4
    assert BLK == 16 and SUP == 8 and D == 512 and B == 2

    x_blk = x.rearrange("b (p t) d -> b p t d", t=BLK)
    out_blk = out.rearrange("b (p t) d -> b p t d", t=BLK)
    spk_blk = spikes_dram.rearrange("(b p t) d -> b p t d", b=B, t=BLK)
    x_rows = x.rearrange("b s d -> (b s) d")
    out_rows = out.rearrange("b s d -> (b s) d")

    def piece(q):
        return slice(q * TQ, (q + 1) * TQ)

    with ExitStack() as ctx:
        def sb(name, shape, dt=F32):
            return ctx.enter_context(nc.sbuf_tensor(name, shape, dt))

        def sem(name):
            return ctx.enter_context(nc.semaphore(name))

        def psum(name):
            return ctx.enter_context(nc.psum_tensor(name, [P, 512], F32))

        x_keep = sb("x_keep", [P, BLK, D])
        acc = [sb(f"acc{b}", [P, BLK, D]) for b in range(B)]
        w1_sb = sb("w1_sb", [P, DC, F])
        w2_sb = sb("w2_sb", [P, FC, D])
        b1_rows = sb("b1_rows", [FC, P])
        b1_col = sb("b1_col", [P, FC])
        relu_b1 = sb("relu_b1", [P, FC])
        b2_all = sb("b2_all", [P, D])
        idle_row = sb("idle_row", [P, D])
        init_all = sb("init_all", [P, B, D])
        ident = sb("ident", [P, P])
        upper = sb("upper", [P, P])
        ones = sb("ones", [P, P])
        block_keep = sb("block_keep", [P, DC * P], BF16)
        group_keep = sb("group_keep", [P, DC * SUP], BF16)
        level1 = sb("level1", [P, DC * P])
        level2 = sb("level2", [P, DC * SUP])
        level2_before = sb("level2_before", [P, DC, SUP + 1])
        block_sum = sb("block_sum", [P, DC, P + 1])
        near_start = level1[0:1, :].bitcast(I32)
        first_prev = sb("first_prev", [P, D])
        nearest = [sb(f"nearest{i}", [P, TQ, D], I32) for i in range(2)]
        slot_hot = nearest[0][:, :, :].rearrange("p t d -> p (t d)").bitcast(BF16).rearrange("p (t k) -> p t k", k=P)
        tile_hot = nearest[1][:, :, :].rearrange("p t d -> p (t d)").bitcast(BF16)[:, 0:TOK * 3 * NT].rearrange(
            "p (t a k) -> p t a k", a=3, k=NT)
        spike_size = sb("spike_size", [P, TOK])
        is_kind = sb("is_kind", [P, 2, TOK])
        kind_run = sb("kind_run", [P, 2, TOK])
        tiles_kind = sb("tiles_kind", [P, 2], I32)
        general_tiles = sb("general_tiles", [P, 1])
        singles_before = sb("singles_before", [P, 1])
        eighth = sb("eighth", [P, 1])
        rank_f = sb("rank_f", [P, 2, TOK])
        rank_i = sb("rank_i", [P, TOK], I32)
        rank_tile = sb("rank_tile", [P, TOK], I32)
        rank_slot = sb("rank_slot", [P, TOK], I32)
        slot_b = sb("slot_b", [P, TOK], BF16)
        tile_b = sb("tile_b", [P, TOK], BF16)
        iota_i = sb("iota_i", [P, P], I32)
        iota_b = sb("iota_b", [P, P], BF16)
        part_i = sb("part_i", [P, 1], I32)
        part_f = sb("part_f", [P, B])
        found = sb("found", [P, 3, NT])
        row_id = sb("row_id", [P, NT])
        missing = sb("missing", [P, NT])
        gather_at = sb("gather_at", [P, 2 * NT + 2], I32)
        scatter_at = sb("scatter_at", [P, 2 * NT + 2], I32)
        gather_col = [sb(f"gather_col{i}", [P, 1], I32) for i in range(2)]
        scatter_col = sb("scatter_col", [P, 1], I32)
        single_col = [sb(f"single_col{i}", [P, 1], I32) for i in range(RING)]
        single_to = [sb(f"single_to{i}", [P, 1], I32) for i in range(RING)]
        key_f = [sb(f"key_f{i}", [P, 1]) for i in range(RING)]
        key_i = [sb(f"key_i{i}", [P, 1], I32) for i in range(RING)]
        hidden = sb("hidden", [P, FC, P])
        table_hidden = [hidden[:, i * DC:(i + 1) * DC, :] for i in range(2)]
        table_row = [hidden[:, c * DC:(c + 1) * DC, :].rearrange("p c k -> p (c k)") for c in range(DC)]
        ffn = sb("ffn", [P, D])
        last_floor = ffn
        spk_rows = [acc[1][:, i, :] for i in range(2)]
        x_got = [acc[1][:, 2 + i, :] for i in range(2)]
        spk_t = acc[1][:, 4, :].rearrange("p (c k) -> p c k", c=DC)
        single_spk = [acc[1][:, 5 + i, :] for i in range(2)]
        single_x = [acc[1][:, 7 + i, :] for i in range(RING)]
        table_got = [acc[1][:, 11 + i, :] for i in range(RING)]
        channel = init_all[:, 0, :]
        junk = table_row[3]

        ps_turn = psum("ps_turn")
        ps_before = psum("ps_before")
        ps_small = psum("ps_small")
        ps_table = [psum(f"ps_table{c}") for c in range(DC)]
        ps_idle = ps_out = ps_table[0]
        ps_hidden = [ps_table[1], ps_table[2]]
        ps_spk = psum("ps_spk")
        ps_list = ps_small[:, 64:64 + 3 * NT]

        x_in = [[sem(f"x_in{b}_{q}") for q in range(XQ)] for b in range(B)]
        init_in = sem("init_in")
        w1_in = [sem(f"w1_in{i}") for i in range(2)]
        w2_in = sem("w2_in")
        b1_in = sem("b1_in")
        b2_in = sem("b2_in")
        const_ready = sem("const_ready")
        pool_step = sem("pool_step")
        dve_step = sem("dve_step")
        rates_ready = sem("rates_ready")
        sums_ready = [sem(f"sums_ready{b}") for b in range(B)]
        totals_turned = sem("totals_turned")
        before_ready = sem("before_ready")
        before_turned = sem("before_turned")
        sum_ready = sem("sum_ready")
        nearest_ready = sem("nearest_ready")
        floors_ready = sem("floors_ready")
        edge_copied = sem("edge_copied")
        edge_in = [sem(f"edge_in{b}") for b in range(B)]
        pool_spikes = [sem(f"pool_spikes{b}") for b in range(B)]
        dve_spikes = sem("dve_spikes")
        size_summed = sem("size_summed")
        spikes_stored = [sem(f"spikes_stored{b}") for b in range(B)]
        b1_turned = sem("b1_turned")
        b1_ready = sem("b1_ready")
        idle_summed = sem("idle_summed")
        idle_ready = sem("idle_ready")
        idle_added = [sem(f"idle_added{b}") for b in range(B)]
        idle_stored = sem("idle_stored")
        x_again = sem("x_again")
        w1_turned = sem("w1_turned")
        table_hidden_ready = sem("table_hidden_ready")
        table_summed = sem("table_summed")
        table_rows_ready = sem("table_rows_ready")
        table_stored = sem("table_stored")
        kinds_counted = sem("kinds_counted")
        kinds_before = sem("kinds_before")
        hots_ready = sem("hots_ready")
        found_ready = sem("found_ready")
        list_ready = sem("list_ready")
        spk_got = [sem(f"spk_got{i}") for i in range(2)]
        xrow_got = [sem(f"xrow_got{i}") for i in range(2)]
        spk_turned = sem("spk_turned")
        spk_copied = sem("spk_copied")
        hidden_summed = sem("hidden_summed")
        hidden_ready = sem("hidden_ready")
        out_summed = sem("out_summed")
        ffn_ready = sem("ffn_ready")
        col_copied = sem("col_copied")
        row_added = sem("row_added")
        ffn_used = sem("ffn_used")
        scattered = sem("scattered")
        single_spk_got = [sem(f"single_spk_got{i}") for i in range(2)]
        single_x_got = [sem(f"single_x_got{i}") for i in range(RING)]
        key_summed = sem("key_summed")
        key_ready = sem("key_ready")
        table_row_got = [sem(f"table_row_got{i}") for i in range(RING)]
        single_summed = sem("single_summed")
        single_scattered = [sem(f"single_scattered{i}") for i in range(RING)]
        passed = sem("passed")
        channel_ready = sem("channel_ready")

        LAST_DVE = TQ
        LOW = [0, LAST_DVE + 1]

        def spikes_done(eng, b, t):
            if b == 1 and t <= LAST_DVE:
                eng.wait_ge(dve_spikes, LAST_DVE + 1 - t)
            else:
                eng.wait_ge(pool_spikes[b], BLK - t)

        TOTALS_AT = 1
        BEFORE_AT = 4

        def over_pairs(eng, end, step):
            with eng.If(end > 0):
                with eng.Fori(0, (end + 1) // 2) as pair:
                    for side in range(2):
                        tile = pair * 2 + side
                        with eng.If(tile < end):
                            step(tile, pair, side)

        block = ctx.enter_context(nc.Block())

        @block.sync
        def _(sp):
            for q in range(XQ):
                sp.dma_start(x_keep[:, piece(q), :], x_blk[0, :, piece(q), :]).then_inc(x_in[0][q], 16)
            sp.dma_start(b1_rows[:, :], b1.rearrange("(c p) -> c p", p=P)).then_inc(b1_in, 16)
            sp.dma_start(init_all[:, :, :], cond.rearrange("(o b) d -> o b d", o=1).to_broadcast([P, B, D])).then_inc(init_in, 16)
            sp.dma_start(b2_all[:, :], b2.rearrange("(o d) -> o d", o=1).to_broadcast([P, D])).then_inc(b2_in, 16)
            sp.dma_start(w2_sb[:, :, :], w2.rearrange("(c p) d -> p c d", p=P)).then_inc(w2_in, 16)

            def load_second(q):
                sp.dma_start(acc[1][:, piece(q), :], x_blk[1, :, piece(q), :]).then_inc(x_in[1][q], 16)

            def load_w1(half):
                part = slice(half * (F // 2), (half + 1) * (F // 2))
                sp.dma_start(w1_sb[:, :, part], w1.rearrange("(c p) f -> p c f", p=P)[:, :, part]).then_inc(w1_in[half], 16)

            load_second(0)
            load_second(1)
            load_w1(0)
            load_second(2)
            load_second(3)
            load_w1(1)

            def next_block(b):
                sp.wait_ge(edge_copied, b + 1)
                if b == 1:
                    sp.wait_ge(pool_spikes[0], BLK)
                sp.dma_start(first_prev[1:P, :], last_floor[0:P - 1, :]).then_inc(edge_in[b], 16)

            def store_spikes(b, q):
                spikes_done(sp, b, q * TQ)
                sp.dma_start(spk_blk[b, :, piece(q), :], acc[b][:, piece(q), :]).then_inc(spikes_stored[b], 16)

            def store_idle(b, q):
                sp.wait_ge(idle_added[b], q + 1)
                buf = x_keep if b == 0 else acc[0]
                sp.dma_start(out_blk[b, :, piece(q), :], buf[:, piece(q), :]).then_inc(idle_stored, 16)

            next_block(0)
            for q in range(XQ - 1, -1, -1):
                store_spikes(0, q)
            sp.wait_ge(spikes_stored[0], 16 * XQ)
            sp.wait_ge(size_summed, BLK)
            sp.dma_start(acc[0][:, :, :], x_blk[1]).then_inc(x_again, 16)
            store_idle(0, 0)
            next_block(1)
            store_spikes(1, 3)
            store_idle(0, 1)
            for q in range(2, -1, -1):
                store_spikes(1, q)
            store_idle(0, 2)
            store_idle(0, 3)
            for c in range(DC):
                sp.wait_ge(table_rows_ready, c + 1)
                sp.dma_start(table_dram[c * P:(c + 1) * P, :], table_row[c]).then_inc(table_stored, 16)
            for q in range(XQ):
                store_idle(1, q)
            sp.wait_ge(idle_stored, 16 * B * XQ)
            sp.wait_ge(table_stored, 16 * DC)

        @block.gpsimd
        def _(pool):
            steps = [0]

            def chain(ins):
                steps[0] += 1
                ins.then_inc(pool_step, 1)
                pool.wait_ge(pool_step, steps[0])

            chain(pool.memset(ident[:, :], 0.0))
            chain(pool.memset(ones[:, :], 1.0))
            pool.affine_select(out=ident[:, :], in_=ident[:, :], compare_op=ALU.not_equal, fill=1.0, base=0,
                               pattern=[[-1, P]], channel_multiplier=1).then_inc(const_ready, 1)
            pool.affine_select(out=upper[:, :], in_=ones[:, :], compare_op=ALU.is_gt, fill=0.0, base=0,
                               pattern=[[1, P]], channel_multiplier=-1).then_inc(const_ready, 1)
            pool.iota(iota_i[:, :], pattern=[[1, P]], base=0, channel_multiplier=0).then_inc(const_ready, 1)
            pool.iota(part_i[:, :], pattern=[[1, 1]], base=0, channel_multiplier=1).then_inc(const_ready, 1)

            pool.sem_inc(ffn_used, 1)
            pool.sem_inc(single_summed, 1)

            for t in range(1, BLK):
                pool.wait_ge(rates_ready, XQ + t // TQ + 1)
                last = pool.tensor_tensor(acc[1][:, t, :], acc[1][:, t, :], acc[1][:, t - 1, :], ALU.add)
                if t < BLK - 1:
                    chain(last)
            last.then_inc(sums_ready[1], 1)

            def spikes(b, first, last):
                for t in range(first, last - 1, -1):
                    if t > 0:
                        pool.wait_ge(floors_ready, XQ * b + XQ - (t - 1) // TQ)
                    if t == BLK - 1:
                        pool.wait_ge(edge_copied, b + 1)
                    if t == 0:
                        pool.wait_ge(edge_in[b], 16)
                    before = acc[b][:, t - 1, :] if t > 0 else first_prev[:, :]
                    pool.tensor_tensor(acc[b][:, t, :], acc[b][:, t, :], before, ALU.subtract).then_inc(pool_spikes[b], 1)
                    pool.wait_ge(pool_spikes[b], BLK - t)

            def add_idle(b, q):
                buf = x_keep if b == 0 else acc[0]
                for t in range(q * TQ, (q + 1) * TQ):
                    last = pool.tensor_tensor(buf[:, t, :], buf[:, t, :], idle_row[:, :], ALU.add)
                last.then_inc(idle_added[b], 1)

            spikes(0, BLK - 1, 0)
            pool.wait_ge(sum_ready, XQ)
            pool.iota(channel.bitcast(I32), pattern=[[1, D]], base=0, channel_multiplier=0).then_inc(channel_ready, 1)
            pool.wait_ge(idle_ready, 1)
            add_idle(0, 0)
            spikes(1, BLK - 1, 3 * TQ + 1)
            add_idle(0, 1)
            spikes(1, 3 * TQ, 2 * TQ + 1)
            spikes(1, 2 * TQ, LOW[1])
            add_idle(0, 2)
            add_idle(0, 3)

            pool.wait_ge(list_ready, 2)
            general = pool.value_load(tiles_kind[0:1, 0:1], min_val=0, max_val=NT - 1)
            singles = pool.value_load(tiles_kind[0:1, 1:2], min_val=0, max_val=NT - 1)
            last_row = pool.to_reg(ROWS - 1)
            pool.wait_ge(spikes_stored[0], 16 * XQ)
            pool.wait_ge(spikes_stored[1], 16 * XQ)

            def gather(tile, side):
                pool.tensor_copy(gather_col[side][:, :], gather_at[:, bass.ds(tile, 1)]).then_inc(col_copied, 1)
                pool.wait_ge(col_copied, 1)
                pool.sem_clear(col_copied)
                at = bass.IndirectOffsetOnAxis(ap=gather_col[side][:, :], axis=0)
                pool.indirect_dma_start(out=spk_rows[side], out_offset=None,
                                        in_=spikes_dram, in_offset=at).then_inc(spk_got[side], 16)
                pool.indirect_dma_start(out=x_got[side], out_offset=None,
                                        in_=x_rows, in_offset=at).then_inc(xrow_got[side], 16)

            with pool.If(general > 0):
                gather(0, 0)
            with pool.If(general > 1):
                gather(1, 1)

            def single_begin(tile, group, side):
                with pool.If(group >= 1):
                    pool.wait_ge(single_scattered[side], group * 16)
                pool.tensor_copy(single_col[side][:, :], gather_at[:, bass.ds(general + tile, 1)]).then_inc(col_copied, 1)
                pool.tensor_copy(single_to[side][:, :], scatter_at[:, bass.ds(general + tile, 1)]).then_inc(col_copied, 1)
                pool.wait_ge(col_copied, 2)
                pool.sem_clear(col_copied)
                at = bass.IndirectOffsetOnAxis(ap=single_col[side][:, :], axis=0)
                pool.indirect_dma_start(out=single_spk[side % 2], out_offset=None,
                                        in_=spikes_dram, in_offset=at).then_inc(single_spk_got[side % 2], 16)
                pool.indirect_dma_start(out=single_x[side], out_offset=None,
                                        in_=x_rows, in_offset=at).then_inc(single_x_got[side], 16)

            def single_look_up(tile, side):
                side = (side - 1) % RING
                pool.wait_ge(key_ready, tile)
                pool.sem_inc(passed, 1)
                pool.indirect_dma_start(out=table_got[side], out_offset=None, in_=table_dram,
                                        in_offset=bass.IndirectOffsetOnAxis(ap=key_i[side][:, :], axis=0)
                                        ).then_inc(table_row_got[side], 16)

            def single_scatter(tile, side):
                side = (side - 2) % RING
                pool.wait_ge(single_summed, tile)
                pool.sem_inc(passed, 1)
                pool.indirect_dma_start(
                    out=out_rows, out_offset=bass.IndirectOffsetOnAxis(ap=single_to[side][:, :], axis=0),
                    in_=single_x[side], in_offset=None, bounds_check=last_row,
                    oob_is_err=False).then_inc(single_scattered[side], 16)

            pool.wait_ge(table_stored, 16 * DC)
            pool.wait_ge(idle_stored, 16 * B * XQ)
            with pool.If(singles > 0):
                with pool.Fori(0, (singles + 2 + RING - 1) // RING) as group:
                    for side in range(RING):
                        tile = group * RING + side
                        with pool.If(tile < singles):
                            single_begin(tile, group, side)
                        with pool.If(tile >= 1):
                            with pool.If(tile < singles + 1):
                                single_look_up(tile, side)
                        with pool.If(tile >= 2):
                            with pool.If(tile < singles + 2):
                                single_scatter(tile, side)

            def finish(tile, pair, side):
                pool.wait_ge(xrow_got[side], pair * 16 + 16)
                pool.tensor_tensor(x_got[side], x_got[side], b2_all[:, :], ALU.add).then_inc(row_added, 1)
                pool.tensor_copy(scatter_col[:, :], scatter_at[:, bass.ds(tile, 1)]).then_inc(row_added, 1)
                pool.wait_ge(row_added, 2)
                pool.wait_ge(ffn_ready, tile + 1)
                pool.tensor_tensor(x_got[side], ffn[:, :], x_got[side], ALU.add).then_inc(row_added, 1)
                pool.wait_ge(row_added, 3)
                pool.sem_clear(row_added)
                pool.sem_inc(ffn_used, 1)
                pool.indirect_dma_start(
                    out=out_rows, out_offset=bass.IndirectOffsetOnAxis(ap=scatter_col[:, :], axis=0),
                    in_=x_got[side], in_offset=None, bounds_check=last_row,
                    oob_is_err=False).then_inc(scattered, 16)
                pool.wait_ge(scattered, pair * 32 + side * 16 + 16)
                with pool.If(tile + 2 < general):
                    gather(tile + 2, side)

            over_pairs(pool, general, finish)
            for side in range(RING):
                with pool.If(singles > side):
                    pool.wait_ge(single_scattered[side], (singles + RING - 1 - side) // RING * 16)
                pool.sem_inc(passed, 1)

        @block.scalar
        def _(act):
            def rates(b, q):
                src = x_keep if b == 0 else acc[1]
                act.wait_ge(x_in[b][q], 16)
                act.activation(acc[b][:, piece(q), :], src[:, piece(q), :], ACT.Relu, scale=DT).then_inc(rates_ready, 1)

            def near(b, q):
                i = b * XQ + XQ - 1 - q
                act.wait_ge(sum_ready, i + 1)
                if i >= 2:
                    act.wait_ge(floors_ready, i - 1)
                act.activation(nearest[i % 2][:, :, :], acc[b][:, piece(q), :], ACT.Copy).then_inc(nearest_ready, 1)

            def copy_edge(b):
                act.wait_ge(floors_ready, b * XQ + 1)
                if b > 0:
                    act.wait_ge(edge_in[b - 1], 16)
                act.activation(last_floor[:, :], acc[b][:, BLK - 1, :], ACT.Copy).then_inc(edge_copied, 1)

            def sizes(b, first, last):
                for t in range(first, last - 1, -1):
                    spikes_done(act, b, t)
                    act.activation(junk, acc[b][:, t, :], ACT.Square, bias=eighth[:, 0:1],
                                   accum_out=spike_size[:, b * BLK + t:b * BLK + t + 1]).then_inc(size_summed, 1)
                    act.wait_ge(size_summed, b * BLK + BLK - t)

            def table_chunk(m):
                act.wait_ge(w1_turned, m + 1)
                if m >= 2:
                    act.wait_ge(table_summed, m - 1)
                act.activation(table_hidden[m % 2], ps_spk[:, :].rearrange("p (c k) -> p c k", c=DC), ACT.Relu,
                               bias=b1_col[:, m:m + 1], scale=PER_DT).then_inc(table_hidden_ready, 1)

            for q in range(XQ):
                rates(0, q)
            act.wait_ge(b1_turned, 1)
            act.activation(b1_col[:, :], ps_small[:, 0:FC], ACT.Copy).then_inc(b1_ready, 1)
            act.wait_ge(b1_ready, 1)
            act.activation(relu_b1[:, :], b1_col[:, :], ACT.Relu).then_inc(b1_ready, 1)
            rates(1, 0)
            rates(1, 1)
            near(0, 3)
            near(0, 2)
            copy_edge(0)
            act.wait_ge(idle_summed, 1)
            act.activation(idle_row[:, :], ps_idle[:, :], ACT.Copy).then_inc(idle_ready, 1)
            table_chunk(0)
            rates(1, 2)
            rates(1, 3)
            near(0, 1)
            table_chunk(1)
            table_chunk(2)
            near(0, 0)
            table_chunk(3)
            sizes(0, 15, 12)
            table_chunk(4)
            sizes(0, 11, 8)
            table_chunk(5)
            act.wait_ge(channel_ready, 1)
            act.activation(channel, channel.bitcast(I32), ACT.Copy).then_inc(channel_ready, 1)
            near(1, 3)
            sizes(0, 7, 4)
            table_chunk(6)
            sizes(0, 3, 0)
            near(1, 2)
            table_chunk(7)
            copy_edge(1)
            table_chunk(8)
            near(1, 1)
            table_chunk(9)
            sizes(1, 15, 13)
            table_chunk(10)
            near(1, 0)
            sizes(1, 12, 9)
            table_chunk(11)
            sizes(1, 8, 5)
            table_chunk(12)
            sizes(1, 4, 0)
            table_chunk(13)
            table_chunk(14)
            table_chunk(15)
            act.wait_ge(table_summed, FC)
            for c in range(DC):
                act.activation(table_row[c], ps_table[c][:, :], ACT.Copy).then_inc(table_rows_ready, 1)

            def copy_spikes(t):
                act.wait_ge(spk_turned, t + 1)
                act.activation(spk_t, ps_spk[:, :].rearrange("p (c k) -> p c k", c=DC), ACT.Copy).then_inc(spk_copied, 1)

            def evacuate(t, end):
                for m in range(FC):
                    act.wait_ge(hidden_summed, t * FC + m + 1)
                    act.activation(hidden[:, m, :], ps_hidden[m % 2][:, 0:P], ACT.Relu,
                                   bias=b1_col[:, m:m + 1], scale=PER_DT).then_inc(hidden_ready, 1)
                with act.If(t + 1 < end):
                    copy_spikes(t + 1)
                act.wait_ge(out_summed, t + 1)
                act.wait_ge(ffn_used, t + 1)
                act.activation(ffn[:, :], ps_out[:, :], ACT.Copy).then_inc(ffn_ready, 1)

            act.wait_ge(list_ready, 2)
            general = act.value_load(tiles_kind[0:1, 0:1], min_val=0, max_val=NT - 1)
            act.wait_ge(table_stored, 16 * DC)
            act.wait_ge(edge_in[1], 16)
            with act.If(general > 0):
                copy_spikes(0)
                with act.Fori(0, general) as t:
                    evacuate(t, general)

        @block.vector
        def _(dve):
            steps = [0]

            def chain(ins):
                steps[0] += 1
                ins.then_inc(dve_step, 1)
                dve.wait_ge(dve_step, steps[0])

            dve.memset(block_keep[:, :], 1.0)
            dve.memset(eighth[:, :], 0.125)
            chain(dve.memset(group_keep[:, :], 1.0))
            dve.memset(block_keep[:, :].rearrange("p (g k) -> p g k", k=BLK)[:, :, 0:1], 0.0)
            dve.memset(group_keep[:, :].rearrange("p (c g) -> p c g", g=SUP)[:, :, 0:1], 0.0)
            dve.memset(level2_before[:, :, 0:1], 0.0)
            chain(dve.memset(block_sum[:, :, 0:1], 0.0))
            for t in range(1, BLK):
                dve.wait_ge(rates_ready, t // TQ + 1)
                last = dve.tensor_tensor(acc[0][:, t, :], acc[0][:, t, :], acc[0][:, t - 1, :], ALU.add)
                if t < BLK - 1:
                    chain(last)
            last.then_inc(sums_ready[0], 1)

            def block_prefix(b):
                dve.wait_ge(totals_turned, b + 1)
                chain(dve.tensor_tensor_scan(level1[:, :], block_keep[:, :], ps_turn[:, :], 0.0, ALU.mult, ALU.add))
                groups = level1[:, :].rearrange("p (c k) -> p c k", k=BLK)
                chain(dve.tensor_tensor_scan(level2[:, :], group_keep[:, :], groups[:, :, BLK - 1], 0.0,
                                             ALU.mult, ALU.add))
                chain(dve.tensor_copy(level2_before[:, :, 1:SUP + 1], level2[:, :].rearrange("p (c g) -> p c g", g=SUP)))
                dve.tensor_tensor(
                    block_sum[:, :, 1:P + 1].rearrange("p c (g k) -> p c g k", k=BLK),
                    level1[:, :].rearrange("p (c g k) -> p c g k", g=SUP, k=BLK),
                    level2_before[:, :, 0:SUP].rearrange("p c (g o) -> p c g o", o=1).to_broadcast([P, DC, SUP, BLK]),
                    ALU.add).then_inc(before_ready, 1)

            def four(ap):
                return ap.rearrange("p (o d) -> p o d", o=1).to_broadcast([P, TQ, D])

            def add_before(b, q):
                tokens = acc[b][:, piece(q), :]
                chain(dve.tensor_tensor(tokens, tokens, four(ps_before[:, :]), ALU.add))
                dve.tensor_tensor(tokens, tokens, four(init_all[:, b, :]), ALU.add).then_inc(sum_ready, 1)

            def floor(b, q):
                i = b * XQ + XQ - 1 - q
                tokens = acc[b][:, piece(q), :]
                dve.wait_ge(nearest_ready, i + 1)
                chain(dve.tensor_tensor(tokens, nearest[i % 2][:, :, :], tokens, ALU.is_gt))
                dve.tensor_tensor(tokens, nearest[i % 2][:, :, :], tokens, ALU.subtract).then_inc(floors_ready, 1)

            def start_floor(b):
                start = init_all[0:1, b, :]
                chain(dve.tensor_copy(near_start, start))
                chain(dve.tensor_tensor(first_prev[0:1, :], near_start, start, ALU.is_gt))
                chain(dve.tensor_tensor(first_prev[0:1, :], near_start, first_prev[0:1, :], ALU.subtract))

            dve.wait_ge(init_in, 16)
            start_floor(0)
            for b in range(B):
                block_prefix(b)
                dve.wait_ge(before_turned, b + 1)
                for q in range(XQ - 1, -1, -1):
                    add_before(b, q)
                    if q < XQ - 1:
                        floor(b, q + 1)
                floor(b, 0)

            dve.wait_ge(pool_spikes[0], BLK)
            start_floor(1)
            dve.wait_ge(pool_spikes[1], BLK - LOW[1])
            for t in range(LAST_DVE, -1, -1):
                if t == 0:
                    dve.wait_ge(edge_in[1], 16)
                before = acc[1][:, t - 1, :] if t > 0 else first_prev[:, :]
                dve.tensor_tensor(acc[1][:, t, :], acc[1][:, t, :], before, ALU.subtract).then_inc(dve_spikes, 1)
                dve.wait_ge(dve_spikes, LAST_DVE + 1 - t)

            dve.wait_ge(const_ready, 4)
            dve.tensor_copy(iota_b[:, :], iota_i[:, :])
            chain(dve.tensor_copy(part_f[:, 0:1], part_i[:, :]))
            chain(dve.tensor_scalar(part_f[:, 1:2], part_f[:, 0:1], float(P), None, ALU.add))

            dve.wait_ge(size_summed, B * BLK)
            chain(dve.tensor_scalar(rank_f[:, 0, :], spike_size[:, :], 9.4, None, ALU.is_lt))
            chain(dve.scalar_tensor_tensor(out=is_kind[:, 1, :], in0=spike_size[:, :], scalar=9.1, in1=rank_f[:, 0, :],
                                           op0=ALU.is_gt, op1=ALU.mult))
            chain(dve.scalar_tensor_tensor(out=is_kind[:, 0, :], in0=spike_size[:, :], scalar=8.1, in1=is_kind[:, 1, :],
                                           op0=ALU.is_gt, op1=ALU.subtract))
            for k in range(2):
                last = dve.tensor_tensor_scan(kind_run[:, k, :], ones[:, 0:TOK], is_kind[:, k, :], 0.0, ALU.mult, ALU.add)
            last.then_inc(kinds_counted, 1)

            dve.wait_ge(kinds_before, 1)
            chain(dve.tensor_scalar(tiles_kind[:, :], ps_small[:, 2:4], float(P - 1), None, ALU.add))
            dve.scalar_tensor_tensor(out=rank_f[:, 0, :], in0=kind_run[:, 0, :], scalar=ps_small[:, 0:1],
                                     in1=is_kind[:, 0, :], op0=ALU.add, op1=ALU.mult)
            chain(dve.tensor_scalar(tiles_kind[:, :], tiles_kind[:, :], 7, None, ALU.arith_shift_right))
            chain(dve.tensor_copy(general_tiles[:, :], tiles_kind[:, 0:1]))
            chain(dve.scalar_tensor_tensor(out=singles_before[:, :], in0=general_tiles[:, :], scalar=float(P),
                                           in1=ps_small[:, 1:2], op0=ALU.mult, op1=ALU.add))
            chain(dve.scalar_tensor_tensor(out=rank_f[:, 1, :], in0=kind_run[:, 1, :], scalar=singles_before[:, 0:1],
                                           in1=is_kind[:, 1, :], op0=ALU.add, op1=ALU.mult))
            chain(dve.scalar_tensor_tensor(out=rank_i[:, :], in0=rank_f[:, 0, :], scalar=-1.0, in1=rank_f[:, 1, :],
                                           op0=ALU.add, op1=ALU.add))
            dve.tensor_scalar(rank_tile[:, :], rank_i[:, :], 7, None, ALU.arith_shift_right)
            chain(dve.tensor_scalar(rank_slot[:, :], rank_i[:, :], P - 1, None, ALU.bitwise_and))
            dve.tensor_copy(tile_b[:, :], rank_tile[:, :])
            chain(dve.tensor_copy(slot_b[:, :], rank_slot[:, :]))

            def over(ap, n):
                return ap.rearrange("p (t o) -> p t o", o=1).to_broadcast([P, ap.shape[1], n])

            def along(ap, m):
                return ap.rearrange("p (o k) -> p o k", o=1).to_broadcast([P, m, ap.shape[1]])

            chain(dve.tensor_tensor(tile_hot[:, :, 0, :], over(tile_b[:, :], NT), along(iota_b[:, 0:NT], TOK), ALU.is_equal))
            for b in range(B):
                own = slice(b * BLK, (b + 1) * BLK)
                dve.tensor_scalar(tile_hot[:, own, 1, :], tile_hot[:, own, 0, :], part_f[:, b:b + 1], None, ALU.mult)
                dve.tensor_tensor(tile_hot[:, own, 2, :], tile_hot[:, own, 0, :], over(iota_b[:, 0:BLK], NT), ALU.mult)
                dve.tensor_tensor(slot_hot[:, own, :], over(slot_b[:, own], P), along(iota_b[:, :], BLK),
                                  ALU.is_equal).then_inc(hots_ready, 1)

            dve.wait_ge(x_again, 16)
            for q in range(XQ):
                tokens = acc[0][:, piece(q), :]
                dve.tensor_tensor(tokens, tokens, four(idle_row[:, :]), ALU.add).then_inc(idle_added[1], 1)

            dve.wait_ge(found_ready, 1)
            chain(dve.tensor_copy(found[:, :, :], ps_list.rearrange("p (a k) -> p a k", k=NT)))
            dve.tensor_scalar(missing[:, :], found[:, 0, :], -float(ROWS), float(ROWS), ALU.mult, ALU.add)
            chain(dve.scalar_tensor_tensor(out=row_id[:, :], in0=found[:, 1, :], scalar=float(BLK),
                                           in1=found[:, 2, :], op0=ALU.mult, op1=ALU.add))
            dve.tensor_copy(gather_at[:, 0:NT], row_id[:, :]).then_inc(list_ready, 1)
            dve.tensor_tensor(scatter_at[:, 0:NT], missing[:, :], row_id[:, :], ALU.add).then_inc(list_ready, 1)

            dve.wait_ge(list_ready, 2)
            singles = dve.value_load(tiles_kind[0:1, 1:2], min_val=0, max_val=NT - 1)
            dve.wait_ge(channel_ready, 2)

            def single_key(group, side):
                dve.wait_ge(single_spk_got[side % 2], group * (16 * RING // 2) + side // 2 * 16 + 16)
                dve.tensor_tensor_reduce(single_spk[side % 2], single_spk[side % 2], channel, 1.0, 0.0, ALU.mult,
                                         ALU.add, key_f[side][:, :]).then_inc(key_summed, 1)
                dve.wait_ge(key_summed, group * RING + side + 1)
                dve.tensor_scalar(key_i[side][:, :], key_f[side][:, :], 0.0, float(D - 1), ALU.max, ALU.min).then_inc(key_ready, 1)

            def single_add(group, side):
                at = group * 16 + (16 if side > 0 else 0)
                side = (side - 1) % RING
                dve.wait_ge(single_x_got[side], at)
                dve.wait_ge(table_row_got[side], at)
                dve.tensor_tensor(single_x[side], single_x[side], table_got[side], ALU.add).then_inc(single_summed, 1)

            with dve.If(singles > 0):
                with dve.Fori(0, (singles + 1 + RING - 1) // RING) as group:
                    for side in range(RING):
                        tile = group * RING + side
                        with dve.If(tile < singles):
                            single_key(group, side)
                        with dve.If(tile >= 1):
                            with dve.If(tile < singles + 1):
                                single_add(group, side)

        @block.tensor
        def _(pe):
            pe.wait_ge(const_ready, 2)

            def turn_totals(b):
                pe.wait_ge(sums_ready[b], 1)
                if b > 0:
                    pe.wait_ge(before_ready, b)
                for c in range(DC):
                    last = pe.transpose(ps_turn[:, c * P:(c + 1) * P], acc[b][:, BLK - 1, c * P:(c + 1) * P], ident[:, :])
                last.then_inc(totals_turned, 1)

            def turn_before(b):
                pe.wait_ge(before_ready, b + 1)
                for c in range(DC):
                    last = pe.transpose(ps_before[:, c * P:(c + 1) * P], block_sum[:, c, 0:P], ident[:, :])
                last.then_inc(before_turned, 1)

            def turn_w1(m):
                if m == 0:
                    pe.wait_ge(w1_in[0], 16)
                else:
                    pe.wait_ge(table_hidden_ready, m)
                if m == FC // 2:
                    pe.wait_ge(w1_in[1], 16)
                for c in range(DC):
                    last = pe.transpose(ps_spk[:, c * P:(c + 1) * P], w1_sb[:, c, m * P:(m + 1) * P], ident[:, :])
                last.then_inc(w1_turned, 1)

            def add_b2(to, stop=False):
                return pe.matmul(to[:, :], ones[0:1, :], b2_all[0:1, :], start=True, stop=stop)

            pe.wait_ge(b1_in, 16)
            pe.transpose(ps_small[:, 0:FC], b1_rows[:, :], ident[0:FC, 0:FC]).then_inc(b1_turned, 1)
            turn_totals(0)
            turn_before(0)
            pe.wait_ge(b2_in, 16)
            pe.wait_ge(b1_ready, 2)
            pe.wait_ge(w2_in, 16)
            add_b2(ps_idle)
            for m in range(FC):
                last = pe.matmul(ps_idle[:, :], relu_b1[:, m:m + 1].to_broadcast([P, P]), w2_sb[:, m, :], start=False, stop=(m == FC - 1))
            last.then_inc(idle_summed, 1)

            for c in range(DC - 1, -1, -1):
                if c == 0:
                    pe.wait_ge(idle_ready, 1)
                add_b2(ps_table[c])
            turn_w1(0)
            for m in range(FC):
                if m + 1 < FC:
                    turn_w1(m + 1)
                pe.wait_ge(table_hidden_ready, m + 1)
                for c in range(DC):
                    last = pe.matmul(ps_table[c][:, :], table_hidden[m % 2][:, c, :], w2_sb[:, m, :], start=False, stop=(m == FC - 1))
                last.then_inc(table_summed, 1)
                if m == TOTALS_AT:
                    turn_totals(1)
                if m == BEFORE_AT:
                    pe.wait_ge(sum_ready, XQ)
                    turn_before(1)

            pe.wait_ge(kinds_counted, 1)
            pe.matmul(ps_small[:, 0:2], upper[:, :], kind_run[:, :, TOK - 1], start=True, stop=True)
            pe.matmul(ps_small[:, 2:4], ones[:, :], kind_run[:, :, TOK - 1], start=True, stop=True).then_inc(kinds_before, 1)
            for j in range(TOK):
                if j % BLK == 0:
                    pe.wait_ge(hots_ready, j // BLK + 1)
                last = pe.matmul(ps_list, slot_hot[:, j, :], tile_hot[:, j, :, :].rearrange("p a k -> p (a k)"),
                                 start=(j == 0), stop=(j == TOK - 1))
            last.then_inc(found_ready, 1)

            def turn_spikes(pair, side):
                pe.wait_ge(spk_got[side], pair * 16 + 16)
                for c in range(DC):
                    last = pe.transpose(ps_spk[:, c * P:(c + 1) * P], spk_rows[side][:, c * P:(c + 1) * P], ident[:, :])
                last.then_inc(spk_turned, 1)

            def ffn_tile(tile, pair, side):
                if side == 0:
                    with pe.If(pair < 1):
                        turn_spikes(0, 0)
                pe.wait_ge(spk_copied, tile + 1)
                for m in range(FC):
                    if m >= 2:
                        pe.wait_ge(hidden_ready, tile * FC + m - 1)
                    for c in range(DC):
                        last = pe.matmul(ps_hidden[m % 2][:, 0:P], w1_sb[:, c, m * P:(m + 1) * P],
                                         spk_t[:, c, :], start=(c == 0), stop=(c == DC - 1))
                    last.then_inc(hidden_summed, 1)
                with pe.If(tile + 1 < general):
                    turn_spikes(pair + side, 1 - side)
                for m in range(FC):
                    pe.wait_ge(hidden_ready, tile * FC + m + 1)
                    last = pe.matmul(ps_out[:, :], hidden[:, m, :], w2_sb[:, m, :],
                                     start=(m == 0), stop=(m == FC - 1))
                last.then_inc(out_summed, 1)

            pe.wait_ge(list_ready, 2)
            general = pe.value_load(tiles_kind[0:1, 0:1], min_val=0, max_val=NT - 1)
            pe.wait_ge(table_rows_ready, DC)
            over_pairs(pe, general, ffn_tile)


def kernel(**inputs):
    import concourse.bacc as bacc
    from concourse.bass_utils import run_bass_kernel_spmd

    nc = bacc.Bacc("TRN2", target_bir_lowering=False, num_devices=1)
    arrays, args = {}, []
    for name in ["x", "cond_1024", "L0_ffn_w1", "L0_ffn_b1", "L0_ffn_w2", "L0_ffn_b2"]:
        a = np.ascontiguousarray(inputs[name])
        arrays[f"in_{name}"] = a
        args.append(nc.dram_tensor(f"in_{name}", a.shape, mybir.dt.from_np(a.dtype), kind="ExternalInput").ap())
    shape = inputs["x"].shape
    spikes = nc.dram_tensor("spikes", (shape[0] * shape[1], shape[2]), F32, kind="Internal").ap()
    table = nc.dram_tensor("table", (shape[2], shape[2]), F32, kind="Internal").ap()
    out = nc.dram_tensor("out", shape, F32, kind="ExternalOutput").ap()
    spike_ffn(nc, *args, spikes, table, out)
    r = run_bass_kernel_spmd(nc, [arrays], core_ids=[0])
    return r.results[0]["out"]
```

```python
from contextlib import ExitStack

import numpy as np
import concourse.bass as bass
from concourse import mybir

ALU = mybir.AluOpType
ACT = mybir.ActivationFunctionType
F32 = mybir.dt.float32
BF16 = mybir.dt.bfloat16
I32 = mybir.dt.int32

P = 128
DT = 0.001
PER_DT = float(np.float32(1.0 / float(np.float32(DT))))


def spike_ffn(nc, x, cond, w1, b1, w2, b2, spikes_dram, table_dram, out):
    B, S, D = x.shape
    F = w1.shape[1]
    BLK = S // P
    DC = D // P
    FC = F // P
    SUP = P // BLK
    TOK = B * BLK
    NT = B * S // P + 1
    ROWS = B * S
    XQ = 4
    TQ = BLK // XQ
    WQ = 4
    RING = 4
    assert BLK == 16 and SUP == 8 and D == 512 and B == 2

    x_blk = x.rearrange("b (p t) d -> b p t d", t=BLK)
    out_blk = out.rearrange("b (p t) d -> b p t d", t=BLK)
    spk_blk = spikes_dram.rearrange("(b p t) d -> b p t d", b=B, t=BLK)
    x_rows = x.rearrange("b s d -> (b s) d")
    out_rows = out.rearrange("b s d -> (b s) d")

    def piece(q):
        return slice(q * TQ, (q + 1) * TQ)

    with ExitStack() as ctx:
        def sb(name, shape, dt=F32):
            return ctx.enter_context(nc.sbuf_tensor(name, shape, dt))

        def sem(name):
            return ctx.enter_context(nc.semaphore(name))

        def psum(name):
            return ctx.enter_context(nc.psum_tensor(name, [P, 512], F32))

        x_keep = sb("x_keep", [P, BLK, D])
        acc = [sb(f"acc{b}", [P, BLK, D]) for b in range(B)]
        w1_sb = sb("w1_sb", [P, DC, F])
        w2_sb = sb("w2_sb", [P, FC, D])
        b1_rows = sb("b1_rows", [FC, P])
        b1_col = sb("b1_col", [P, FC])
        relu_b1 = sb("relu_b1", [P, FC])
        b2_row = sb("b2_row", [1, D])
        idle_row = sb("idle_row", [P, D])
        init_all = sb("init_all", [P, B, D])
        ident = sb("ident", [P, P])
        upper = sb("upper", [P, P])
        ones = sb("ones", [P, P])
        block_keep = sb("block_keep", [P, DC * P], BF16)
        group_keep = sb("group_keep", [P, DC * SUP], BF16)
        level1 = sb("level1", [P, DC * P])
        level2 = sb("level2", [P, DC * SUP])
        level2_before = sb("level2_before", [P, DC, SUP + 1])
        block_sum = sb("block_sum", [P, DC, P + 1])
        first_prev = sb("first_prev", [P, D])
        nearest = [sb(f"nearest{i}", [P, TQ, D], I32) for i in range(2)]
        slot_hot = nearest[0][:, :, :].rearrange("p t d -> p (t d)").bitcast(BF16).rearrange("p (t k) -> p t k", k=P)
        tile_hot = nearest[1][:, :, :].rearrange("p t d -> p (t d)").bitcast(BF16)[:, 0:TOK * 3 * NT].rearrange(
            "p (t a k) -> p t a k", a=3, k=NT)
        spike_size = sb("spike_size", [P, TOK])
        is_kind = sb("is_kind", [P, 2, TOK])
        kind_run = sb("kind_run", [P, 2, TOK])
        tiles_kind = sb("tiles_kind", [P, 2], I32)
        general_tiles = sb("general_tiles", [P, 1])
        singles_before = sb("singles_before", [P, 1])
        eighth = sb("eighth", [P, 1])
        rank_f = sb("rank_f", [P, 2, TOK])
        rank_i = sb("rank_i", [P, TOK], I32)
        rank_tile = sb("rank_tile", [P, TOK], I32)
        rank_slot = sb("rank_slot", [P, TOK], I32)
        slot_b = sb("slot_b", [P, TOK], BF16)
        tile_b = sb("tile_b", [P, TOK], BF16)
        iota_i = sb("iota_i", [P, P], I32)
        iota_b = sb("iota_b", [P, P], BF16)
        part_i = sb("part_i", [P, 1], I32)
        part_f = sb("part_f", [P, B])
        found = sb("found", [P, 3, NT])
        row_id = sb("row_id", [P, NT])
        missing = sb("missing", [P, NT])
        gather_at = sb("gather_at", [P, 2 * NT + 2], I32)
        scatter_at = sb("scatter_at", [P, 2 * NT + 2], I32)
        gather_col = [sb(f"gather_col{i}", [P, 1], I32) for i in range(2)]
        scatter_col = sb("scatter_col", [P, 1], I32)
        single_col = [sb(f"single_col{i}", [P, 1], I32) for i in range(RING)]
        single_to = [sb(f"single_to{i}", [P, 1], I32) for i in range(RING)]
        key_f = [sb(f"key_f{i}", [P, 1]) for i in range(RING)]
        key_i = [sb(f"key_i{i}", [P, 1], I32) for i in range(RING)]
        hidden = sb("hidden", [P, FC, P])
        hidden_row = hidden[0:1, :, :].rearrange("p c k -> p (c k)")
        start_in = hidden_row[:, 0:B * D]
        start_near = hidden_row[:, B * D:2 * B * D].bitcast(I32)
        start_keep = hidden_row[:, B * D:B * D + D]
        table_hidden = [hidden[:, i * DC:(i + 1) * DC, :] for i in range(2)]
        table_row = [nearest[0][:, c, :].bitcast(F32) for c in range(DC)]
        last_floor = sb("last_floor", [P, D])
        spk_rows = [acc[1][:, i, :] for i in range(2)]
        x_got = [acc[1][:, 2 + i, :] for i in range(2)]
        spk_t = acc[1][:, 4, :].rearrange("p (c k) -> p c k", c=DC)
        single_spk = [acc[1][:, 5 + i, :] for i in range(2)]
        single_x = [acc[1][:, 7 + i, :] for i in range(RING)]
        table_got = [acc[1][:, 11 + i, :] for i in range(RING)]
        channel = init_all[:, 0, :]
        junk = hidden[:, 3 * DC:4 * DC, :].rearrange("p c k -> p (c k)")

        ps_turn = psum("ps_turn")
        ps_before = psum("ps_before")
        ps_small = psum("ps_small")
        ps_table = [psum(f"ps_table{c}") for c in range(DC)]
        ps_out = ps_table[0]
        ps_hidden = [ps_table[1], ps_table[2]]
        ps_spk = psum("ps_spk")
        ps_idle = ps_spk
        ps_list = ps_small[:, 64:64 + 3 * NT]

        x_in = [[sem(f"x_in{b}_{q}") for q in range(XQ)] for b in range(B)]
        init_in = sem("init_in")
        start_row_in = sem("start_row_in")
        w1_in = [sem(f"w1_in{i}") for i in range(WQ)]
        w2_in = [sem(f"w2_in{i}") for i in range(WQ)]
        b1_in = sem("b1_in")
        b2_in = sem("b2_in")
        const_ready = sem("const_ready")
        pool_step = sem("pool_step")
        dve_step = sem("dve_step")
        rates_ready = sem("rates_ready")
        sums_ready = [sem(f"sums_ready{b}") for b in range(B)]
        totals_turned = sem("totals_turned")
        before_ready = sem("before_ready")
        before_turned = sem("before_turned")
        sum_ready = sem("sum_ready")
        nearest_ready = sem("nearest_ready")
        floors_ready = sem("floors_ready")
        edge_copied = sem("edge_copied")
        edge_in = [sem(f"edge_in{b}") for b in range(B)]
        pool_spikes = [sem(f"pool_spikes{b}") for b in range(B)]
        dve_spikes = sem("dve_spikes")
        size_summed = sem("size_summed")
        spikes_stored = [sem(f"spikes_stored{b}") for b in range(B)]
        b1_turned = sem("b1_turned")
        b1_ready = sem("b1_ready")
        idle_summed = sem("idle_summed")
        idle_ready = sem("idle_ready")
        idle_added = [sem(f"idle_added{b}") for b in range(B)]
        dve_idle_added = sem("dve_idle_added")
        idle_stored = sem("idle_stored")
        x_again = [sem(f"x_again{q}") for q in range(XQ)]
        w1_turned = sem("w1_turned")
        table_hidden_ready = sem("table_hidden_ready")
        table_summed = sem("table_summed")
        table_rows_ready = sem("table_rows_ready")
        table_stored = sem("table_stored")
        kinds_counted = sem("kinds_counted")
        kinds_before = sem("kinds_before")
        hots_ready = sem("hots_ready")
        found_ready = sem("found_ready")
        list_ready = sem("list_ready")
        spk_got = [sem(f"spk_got{i}") for i in range(2)]
        xrow_got = [sem(f"xrow_got{i}") for i in range(2)]
        spk_turned = sem("spk_turned")
        spk_copied = sem("spk_copied")
        hidden_summed = sem("hidden_summed")
        hidden_ready = sem("hidden_ready")
        out_summed = sem("out_summed")
        col_copied = sem("col_copied")
        row_added = sem("row_added")
        scattered = sem("scattered")
        single_spk_got = [sem(f"single_spk_got{i}") for i in range(2)]
        single_x_got = [sem(f"single_x_got{i}") for i in range(RING)]
        key_summed = sem("key_summed")
        key_ready = sem("key_ready")
        table_row_got = [sem(f"table_row_got{i}") for i in range(RING)]
        single_summed = sem("single_summed")
        single_scattered = [sem(f"single_scattered{i}") for i in range(RING)]
        passed = sem("passed")
        channel_ready = sem("channel_ready")

        LAST_DVE = TQ
        LOW = [0, LAST_DVE + 1]

        def spikes_done(eng, b, t):
            if b == 1 and t <= LAST_DVE:
                eng.wait_ge(dve_spikes, LAST_DVE + 1 - t)
            else:
                eng.wait_ge(pool_spikes[b], BLK - t)

        TOTALS_AT = 0
        BEFORE_AT = 1
        KINDS_AT = 12
        LIST_AT = 14

        def over(ap, n):
            return ap.rearrange("p (t o) -> p t o", o=1).to_broadcast([P, ap.shape[1], n])

        def along(ap, m):
            return ap.rearrange("p (o k) -> p o k", o=1).to_broadcast([P, m, ap.shape[1]])

        def over_pairs(eng, end, step):
            with eng.If(end > 0):
                with eng.Fori(0, (end + 1) // 2) as pair:
                    for side in range(2):
                        tile = pair * 2 + side
                        with eng.If(tile < end):
                            step(tile, pair, side)

        block = ctx.enter_context(nc.Block())

        @block.sync
        def _(sp):
            sp.dma_start(start_in, cond.rearrange("(o b) d -> o (b d)", o=1)).then_inc(start_row_in, 16)
            for q in range(XQ):
                sp.dma_start(x_keep[:, piece(q), :], x_blk[0, :, piece(q), :]).then_inc(x_in[0][q], 16)
            sp.dma_start(b1_rows[:, :], b1.rearrange("(c p) -> c p", p=P)).then_inc(b1_in, 16)
            sp.dma_start(init_all[:, :, :], cond.rearrange("(o b) d -> o b d", o=1).to_broadcast([P, B, D])).then_inc(init_in, 16)
            sp.dma_start(b2_row[:, :], b2.rearrange("(o d) -> o d", o=1)).then_inc(b2_in, 16)

            def load_w2(i):
                part = slice(i * (FC // WQ), (i + 1) * (FC // WQ))
                sp.dma_start(w2_sb[:, part, :], w2.rearrange("(c p) d -> p c d", p=P)[:, part, :]).then_inc(w2_in[i], 16)

            def load_second(q):
                sp.dma_start(acc[1][:, piece(q), :], x_blk[1, :, piece(q), :]).then_inc(x_in[1][q], 16)

            def load_w1(i):
                part = slice(i * (F // WQ), (i + 1) * (F // WQ))
                sp.dma_start(w1_sb[:, :, part], w1.rearrange("(c p) f -> p c f", p=P)[:, :, part]).then_inc(w1_in[i], 16)

            load_w2(0)
            load_w2(1)
            load_second(0)
            load_w2(2)
            load_second(1)
            load_w2(3)
            load_second(2)
            load_second(3)
            for i in range(WQ):
                load_w1(i)

            def next_block(b):
                sp.wait_ge(edge_copied, b + 1)
                if b == 1:
                    sp.wait_ge(pool_spikes[0], BLK)
                sp.dma_start(first_prev[1:P, :], last_floor[0:P - 1, :]).then_inc(edge_in[b], 16)

            def store_spikes(b, q):
                spikes_done(sp, b, q * TQ)
                sp.dma_start(spk_blk[b, :, piece(q), :], acc[b][:, piece(q), :]).then_inc(spikes_stored[b], 16)

            def store_idle(b, q):
                if b == 1 and q > 1:
                    sp.wait_ge(dve_idle_added, q - 1)
                else:
                    sp.wait_ge(idle_added[b], q + 1)
                buf = x_keep if b == 0 else acc[0]
                sp.dma_start(out_blk[b, :, piece(q), :], buf[:, piece(q), :]).then_inc(idle_stored, 16)

            next_block(0)
            store_idle(0, 0)
            for q in range(XQ - 1, -1, -1):
                store_spikes(0, q)
                sp.wait_ge(spikes_stored[0], 16 * (XQ - q))
                sp.wait_ge(size_summed, TQ * (XQ - q))
                sp.dma_start(acc[0][:, piece(q), :], x_blk[1, :, piece(q), :]).then_inc(x_again[q], 16)
            next_block(1)
            store_spikes(1, 3)
            store_idle(0, 1)
            for q in range(2, -1, -1):
                store_spikes(1, q)
            store_idle(0, 2)
            store_idle(0, 3)
            store_idle(1, 0)
            store_idle(1, 1)
            for c in range(DC):
                sp.wait_ge(table_rows_ready, c + 1)
                sp.dma_start(table_dram[c * P:(c + 1) * P, :], table_row[c]).then_inc(table_stored, 16)
            for q in range(2, XQ):
                store_idle(1, q)
            sp.wait_ge(idle_stored, 16 * B * XQ)
            sp.wait_ge(table_stored, 16 * DC)

        @block.gpsimd
        def _(pool):
            steps = [0]

            def chain(ins):
                steps[0] += 1
                ins.then_inc(pool_step, 1)
                pool.wait_ge(pool_step, steps[0])

            chain(pool.memset(ident[:, :], 0.0))
            chain(pool.memset(ones[:, :], 1.0))
            pool.affine_select(out=ident[:, :], in_=ident[:, :], compare_op=ALU.not_equal, fill=1.0, base=0,
                               pattern=[[-1, P]], channel_multiplier=1).then_inc(const_ready, 1)
            pool.affine_select(out=upper[:, :], in_=ones[:, :], compare_op=ALU.is_gt, fill=0.0, base=0,
                               pattern=[[1, P]], channel_multiplier=-1).then_inc(const_ready, 1)
            pool.iota(iota_i[:, :], pattern=[[1, P]], base=0, channel_multiplier=0).then_inc(const_ready, 1)
            pool.iota(part_i[:, :], pattern=[[1, 1]], base=0, channel_multiplier=1).then_inc(const_ready, 1)

            pool.sem_inc(row_added, 1)
            pool.sem_inc(single_summed, 1)

            for t in range(1, BLK):
                pool.wait_ge(rates_ready, XQ + t // TQ + 1)
                last = pool.tensor_tensor(acc[1][:, t, :], acc[1][:, t, :], acc[1][:, t - 1, :], ALU.add)
                if t < BLK - 1:
                    chain(last)
            last.then_inc(sums_ready[1], 1)

            def spikes(b, first, last):
                for t in range(first, last - 1, -1):
                    if t > 0:
                        pool.wait_ge(floors_ready, XQ * b + XQ - (t - 1) // TQ)
                    if t == BLK - 1:
                        pool.wait_ge(edge_copied, b + 1)
                    if t == 0:
                        pool.wait_ge(edge_in[b], 16)
                    before = acc[b][:, t - 1, :] if t > 0 else first_prev[:, :]
                    pool.tensor_tensor(acc[b][:, t, :], acc[b][:, t, :], before, ALU.subtract).then_inc(pool_spikes[b], 1)
                    pool.wait_ge(pool_spikes[b], BLK - t)

            def add_idle(b, first, end):
                buf = x_keep if b == 0 else acc[0]
                for t in range(first, end):
                    ins = pool.tensor_tensor(buf[:, t, :], buf[:, t, :], idle_row[:, :], ALU.add)
                    if t % TQ == TQ - 1:
                        ins.then_inc(idle_added[b], 1)

            pool.wait_ge(idle_ready, 1)
            add_idle(0, 0, TQ)
            spikes(0, BLK - 1, 0)
            pool.wait_ge(sum_ready, XQ)
            pool.iota(channel.bitcast(I32), pattern=[[1, D]], base=0, channel_multiplier=0).then_inc(channel_ready, 1)
            spikes(1, BLK - 1, 3 * TQ + 1)
            add_idle(0, TQ, 2 * TQ)
            spikes(1, 3 * TQ, 2 * TQ + 1)
            add_idle(0, 2 * TQ, 2 * TQ + 2)
            spikes(1, 2 * TQ, LOW[1])
            add_idle(0, 2 * TQ + 2, BLK)
            pool.wait_ge(x_again[0], 16)
            add_idle(1, 0, TQ)
            pool.wait_ge(x_again[1], 16)
            add_idle(1, TQ, 2 * TQ)

            pool.wait_ge(list_ready, 2)
            general = pool.value_load(tiles_kind[0:1, 0:1], min_val=0, max_val=NT - 1)
            singles = pool.value_load(tiles_kind[0:1, 1:2], min_val=0, max_val=NT - 1)
            last_row = pool.to_reg(ROWS - 1)
            pool.wait_ge(spikes_stored[0], 16 * XQ)
            pool.wait_ge(spikes_stored[1], 16 * XQ)

            def gather(tile, side):
                pool.tensor_copy(gather_col[side][:, :], gather_at[:, bass.ds(tile, 1)]).then_inc(col_copied, 1)
                pool.wait_ge(col_copied, 1)
                pool.sem_clear(col_copied)
                at = bass.IndirectOffsetOnAxis(ap=gather_col[side][:, :], axis=0)
                pool.indirect_dma_start(out=spk_rows[side], out_offset=None,
                                        in_=spikes_dram, in_offset=at).then_inc(spk_got[side], 16)
                pool.indirect_dma_start(out=x_got[side], out_offset=None,
                                        in_=x_rows, in_offset=at).then_inc(xrow_got[side], 16)

            with pool.If(general > 0):
                gather(0, 0)
            with pool.If(general > 1):
                gather(1, 1)

            def single_begin(tile, group, side):
                with pool.If(group >= 1):
                    pool.wait_ge(single_scattered[side], group * 16)
                pool.tensor_copy(single_col[side][:, :], gather_at[:, bass.ds(general + tile, 1)]).then_inc(col_copied, 1)
                pool.tensor_copy(single_to[side][:, :], scatter_at[:, bass.ds(general + tile, 1)]).then_inc(col_copied, 1)
                pool.wait_ge(col_copied, 2)
                pool.sem_clear(col_copied)
                at = bass.IndirectOffsetOnAxis(ap=single_col[side][:, :], axis=0)
                pool.indirect_dma_start(out=single_spk[side % 2], out_offset=None,
                                        in_=spikes_dram, in_offset=at).then_inc(single_spk_got[side % 2], 16)
                pool.indirect_dma_start(out=single_x[side], out_offset=None,
                                        in_=x_rows, in_offset=at).then_inc(single_x_got[side], 16)

            def single_look_up(tile, side):
                side = (side - 1) % RING
                pool.wait_ge(key_ready, tile)
                pool.sem_inc(passed, 1)
                pool.wait_ge(table_stored, 16 * DC)
                pool.indirect_dma_start(out=table_got[side], out_offset=None, in_=table_dram,
                                        in_offset=bass.IndirectOffsetOnAxis(ap=key_i[side][:, :], axis=0)
                                        ).then_inc(table_row_got[side], 16)

            def single_scatter(tile, side):
                side = (side - 2) % RING
                pool.wait_ge(single_summed, tile)
                pool.sem_inc(passed, 1)
                pool.wait_ge(idle_stored, 16 * B * XQ)
                pool.indirect_dma_start(
                    out=out_rows, out_offset=bass.IndirectOffsetOnAxis(ap=single_to[side][:, :], axis=0),
                    in_=single_x[side], in_offset=None, bounds_check=last_row,
                    oob_is_err=False).then_inc(single_scattered[side], 16)

            with pool.If(singles > 0):
                with pool.Fori(0, (singles + 2 + RING - 1) // RING) as group:
                    for side in range(RING):
                        tile = group * RING + side
                        with pool.If(tile < singles):
                            single_begin(tile, group, side)
                        with pool.If(tile >= 1):
                            with pool.If(tile < singles + 1):
                                single_look_up(tile, side)
                        with pool.If(tile >= 2):
                            with pool.If(tile < singles + 2):
                                single_scatter(tile, side)

            def finish(tile, pair, side):
                pool.tensor_copy(scatter_col[:, :], scatter_at[:, bass.ds(tile, 1)]).then_inc(col_copied, 1)
                pool.wait_ge(col_copied, 1)
                pool.sem_clear(col_copied)
                pool.wait_ge(row_added, tile + 2)
                pool.sem_inc(passed, 1)
                pool.wait_ge(idle_stored, 16 * B * XQ)
                pool.indirect_dma_start(
                    out=out_rows, out_offset=bass.IndirectOffsetOnAxis(ap=scatter_col[:, :], axis=0),
                    in_=x_got[side], in_offset=None, bounds_check=last_row,
                    oob_is_err=False).then_inc(scattered, 16)
                pool.wait_ge(scattered, pair * 32 + side * 16 + 16)
                pool.sem_inc(passed, 1)
                with pool.If(tile + 2 < general):
                    gather(tile + 2, side)

            over_pairs(pool, general, finish)
            for side in range(RING):
                with pool.If(singles > side):
                    pool.wait_ge(single_scattered[side], (singles + RING - 1 - side) // RING * 16)
                pool.sem_inc(passed, 1)

        @block.scalar
        def _(act):
            def rates(b, q):
                src = x_keep if b == 0 else acc[1]
                act.wait_ge(x_in[b][q], 16)
                act.activation(acc[b][:, piece(q), :], src[:, piece(q), :], ACT.Relu, scale=DT).then_inc(rates_ready, 1)

            def near(b, q):
                i = b * XQ + XQ - 1 - q
                act.wait_ge(sum_ready, i + 1)
                if i >= 2:
                    act.wait_ge(floors_ready, i - 1)
                act.activation(nearest[i % 2][:, :, :], acc[b][:, piece(q), :], ACT.Copy).then_inc(nearest_ready, 1)

            def copy_edge(b):
                act.wait_ge(floors_ready, b * XQ + 1)
                if b > 0:
                    act.wait_ge(edge_in[b - 1], 16)
                act.activation(last_floor[:, :], acc[b][:, BLK - 1, :], ACT.Copy).then_inc(edge_copied, 1)

            def sizes(b, first, last):
                for t in range(first, last - 1, -1):
                    spikes_done(act, b, t)
                    act.activation(junk, acc[b][:, t, :], ACT.Square, bias=eighth[:, 0:1],
                                   accum_out=spike_size[:, b * BLK + t:b * BLK + t + 1]).then_inc(size_summed, 1)
                    act.wait_ge(size_summed, b * BLK + BLK - t)

            def table_chunk(m):
                act.wait_ge(w1_turned, m + 1)
                if m >= 2:
                    act.wait_ge(table_summed, m - 1)
                act.activation(table_hidden[m % 2], ps_spk[:, :].rearrange("p (c k) -> p c k", c=DC), ACT.Relu,
                               bias=b1_col[:, m:m + 1], scale=PER_DT).then_inc(table_hidden_ready, 1)

            for q in range(XQ):
                rates(0, q)
            act.wait_ge(b1_turned, 1)
            act.activation(b1_col[:, :], ps_small[:, 0:FC], ACT.Copy).then_inc(b1_ready, 1)
            act.wait_ge(b1_ready, 1)
            act.activation(relu_b1[:, :], b1_col[:, :], ACT.Relu).then_inc(b1_ready, 1)
            rates(1, 0)
            near(0, 3)
            rates(1, 1)
            near(0, 2)
            copy_edge(0)
            rates(1, 2)
            rates(1, 3)
            near(0, 1)
            act.wait_ge(idle_summed, 1)
            act.activation(idle_row[:, :], ps_idle[:, :], ACT.Copy).then_inc(idle_ready, 1)
            table_chunk(0)
            table_chunk(1)
            near(0, 0)
            table_chunk(2)
            sizes(0, 15, 14)
            table_chunk(3)
            sizes(0, 13, 11)
            table_chunk(4)
            sizes(0, 10, 9)
            near(1, 3)
            table_chunk(5)
            sizes(0, 8, 5)
            near(1, 2)
            table_chunk(6)
            sizes(0, 4, 3)
            copy_edge(1)
            table_chunk(7)
            sizes(0, 2, 0)
            act.wait_ge(channel_ready, 1)
            act.activation(channel, channel.bitcast(I32), ACT.Copy).then_inc(channel_ready, 1)
            near(1, 1)
            table_chunk(8)
            sizes(1, 15, 13)
            table_chunk(9)
            near(1, 0)
            table_chunk(10)
            sizes(1, 12, 9)
            table_chunk(11)
            sizes(1, 8, 7)
            table_chunk(12)
            sizes(1, 6, 0)
            table_chunk(13)
            table_chunk(14)
            table_chunk(15)
            act.wait_ge(table_summed, FC)
            for c in range(DC):
                act.activation(table_row[c], ps_table[c][:, :], ACT.Copy).then_inc(table_rows_ready, 1)

            def copy_spikes(t):
                act.wait_ge(spk_turned, t + 1)
                act.activation(spk_t, ps_spk[:, :].rearrange("p (c k) -> p c k", c=DC), ACT.Copy).then_inc(spk_copied, 1)

            def evacuate(t, end):
                for m in range(FC):
                    act.wait_ge(hidden_summed, t * FC + m + 1)
                    act.activation(hidden[:, m, :], ps_hidden[m % 2][:, 0:P], ACT.Relu,
                                   bias=b1_col[:, m:m + 1], scale=PER_DT).then_inc(hidden_ready, 1)
                with act.If(t + 1 < end):
                    copy_spikes(t + 1)

            act.wait_ge(list_ready, 2)
            general = act.value_load(tiles_kind[0:1, 0:1], min_val=0, max_val=NT - 1)
            with act.If(general > 0):
                copy_spikes(0)
                with act.Fori(0, general) as t:
                    evacuate(t, general)

        @block.vector
        def _(dve):
            steps = [0]

            def chain(ins):
                steps[0] += 1
                ins.then_inc(dve_step, 1)
                dve.wait_ge(dve_step, steps[0])

            dve.memset(block_keep[:, :], 1.0)
            dve.memset(eighth[:, :], 0.125)
            chain(dve.memset(group_keep[:, :], 1.0))
            dve.memset(block_keep[:, :].rearrange("p (g k) -> p g k", k=BLK)[:, :, 0:1], 0.0)
            dve.memset(group_keep[:, :].rearrange("p (c g) -> p c g", g=SUP)[:, :, 0:1], 0.0)
            dve.memset(level2_before[:, :, 0:1], 0.0)
            chain(dve.memset(block_sum[:, :, 0:1], 0.0))
            dve.wait_ge(start_row_in, 16)
            chain(dve.tensor_copy(start_near, start_in))
            chain(dve.tensor_tensor(start_in, start_near, start_in, ALU.is_gt))
            chain(dve.tensor_tensor(first_prev[0:1, :], start_near[:, 0:D], start_in[:, 0:D], ALU.subtract))
            dve.tensor_tensor(start_keep, start_near[:, D:2 * D], start_in[:, D:2 * D], ALU.subtract)
            for t in range(1, BLK):
                dve.wait_ge(rates_ready, t // TQ + 1)
                last = dve.tensor_tensor(acc[0][:, t, :], acc[0][:, t, :], acc[0][:, t - 1, :], ALU.add)
                if t < BLK - 1:
                    chain(last)
            last.then_inc(sums_ready[0], 1)

            def block_prefix(b):
                dve.wait_ge(totals_turned, b + 1)
                chain(dve.tensor_tensor_scan(level1[:, :], block_keep[:, :], ps_turn[:, :], 0.0, ALU.mult, ALU.add))
                groups = level1[:, :].rearrange("p (c k) -> p c k", k=BLK)
                chain(dve.tensor_tensor_scan(level2[:, :], group_keep[:, :], groups[:, :, BLK - 1], 0.0,
                                             ALU.mult, ALU.add))
                chain(dve.tensor_copy(level2_before[:, :, 1:SUP + 1], level2[:, :].rearrange("p (c g) -> p c g", g=SUP)))
                dve.tensor_tensor(
                    block_sum[:, :, 1:P + 1].rearrange("p c (g k) -> p c g k", k=BLK),
                    level1[:, :].rearrange("p (c g k) -> p c g k", g=SUP, k=BLK),
                    level2_before[:, :, 0:SUP].rearrange("p c (g o) -> p c g o", o=1).to_broadcast([P, DC, SUP, BLK]),
                    ALU.add).then_inc(before_ready, 1)

            def four(ap):
                return ap.rearrange("p (o d) -> p o d", o=1).to_broadcast([P, TQ, D])

            def add_before(b, q):
                tokens = acc[b][:, piece(q), :]
                chain(dve.tensor_tensor(tokens, tokens, four(ps_before[:, :]), ALU.add))
                dve.tensor_tensor(tokens, tokens, four(init_all[:, b, :]), ALU.add).then_inc(sum_ready, 1)

            def floor(b, q):
                i = b * XQ + XQ - 1 - q
                tokens = acc[b][:, piece(q), :]
                dve.wait_ge(nearest_ready, i + 1)
                chain(dve.tensor_tensor(tokens, nearest[i % 2][:, :, :], tokens, ALU.is_gt))
                dve.tensor_tensor(tokens, nearest[i % 2][:, :, :], tokens, ALU.subtract).then_inc(floors_ready, 1)

            block_prefix(0)
            dve.wait_ge(init_in, 16)
            for b in range(B):
                dve.wait_ge(before_turned, b + 1)
                for q in range(XQ - 1, -1, -1):
                    add_before(b, q)
                    if b == 0 and q == 0:
                        block_prefix(1)
                    if q < XQ - 1:
                        floor(b, q + 1)
                floor(b, 0)

            dve.wait_ge(pool_spikes[0], BLK)
            chain(dve.tensor_copy(first_prev[0:1, :], start_keep))
            dve.wait_ge(pool_spikes[1], BLK - LOW[1])
            for t in range(LAST_DVE, -1, -1):
                if t == 0:
                    dve.wait_ge(edge_in[1], 16)
                before = acc[1][:, t - 1, :] if t > 0 else first_prev[:, :]
                dve.tensor_tensor(acc[1][:, t, :], acc[1][:, t, :], before, ALU.subtract).then_inc(dve_spikes, 1)
                dve.wait_ge(dve_spikes, LAST_DVE + 1 - t)

            dve.wait_ge(const_ready, 4)
            dve.tensor_copy(iota_b[:, :], iota_i[:, :])
            chain(dve.tensor_copy(part_f[:, 0:1], part_i[:, :]))
            chain(dve.tensor_scalar(part_f[:, 1:2], part_f[:, 0:1], float(P), None, ALU.add))

            dve.wait_ge(size_summed, B * BLK)
            chain(dve.tensor_scalar(rank_f[:, 0, :], spike_size[:, :], 9.4, None, ALU.is_lt))
            chain(dve.scalar_tensor_tensor(out=is_kind[:, 1, :], in0=spike_size[:, :], scalar=9.1, in1=rank_f[:, 0, :],
                                           op0=ALU.is_gt, op1=ALU.mult))
            chain(dve.scalar_tensor_tensor(out=is_kind[:, 0, :], in0=spike_size[:, :], scalar=8.1, in1=is_kind[:, 1, :],
                                           op0=ALU.is_gt, op1=ALU.subtract))
            for k in range(2):
                last = dve.tensor_tensor_scan(kind_run[:, k, :], ones[:, 0:TOK], is_kind[:, k, :], 0.0, ALU.mult, ALU.add)
            last.then_inc(kinds_counted, 1)

            dve.wait_ge(kinds_before, 1)
            chain(dve.tensor_scalar(tiles_kind[:, :], ps_small[:, 2:4], float(P - 1), None, ALU.add))
            dve.scalar_tensor_tensor(out=rank_f[:, 0, :], in0=kind_run[:, 0, :], scalar=ps_small[:, 0:1],
                                     in1=is_kind[:, 0, :], op0=ALU.add, op1=ALU.mult)
            chain(dve.tensor_scalar(tiles_kind[:, :], tiles_kind[:, :], 7, None, ALU.arith_shift_right))
            chain(dve.tensor_copy(general_tiles[:, :], tiles_kind[:, 0:1]))
            chain(dve.scalar_tensor_tensor(out=singles_before[:, :], in0=general_tiles[:, :], scalar=float(P),
                                           in1=ps_small[:, 1:2], op0=ALU.mult, op1=ALU.add))
            chain(dve.scalar_tensor_tensor(out=rank_f[:, 1, :], in0=kind_run[:, 1, :], scalar=singles_before[:, 0:1],
                                           in1=is_kind[:, 1, :], op0=ALU.add, op1=ALU.mult))
            chain(dve.scalar_tensor_tensor(out=rank_i[:, :], in0=rank_f[:, 0, :], scalar=-1.0, in1=rank_f[:, 1, :],
                                           op0=ALU.add, op1=ALU.add))
            dve.tensor_scalar(rank_tile[:, :], rank_i[:, :], 7, None, ALU.arith_shift_right)
            chain(dve.tensor_scalar(rank_slot[:, :], rank_i[:, :], P - 1, None, ALU.bitwise_and))
            dve.tensor_copy(tile_b[:, :], rank_tile[:, :])
            chain(dve.tensor_copy(slot_b[:, :], rank_slot[:, :]))

            chain(dve.tensor_tensor(tile_hot[:, :, 0, :], over(tile_b[:, :], NT), along(iota_b[:, 0:NT], TOK), ALU.is_equal))
            for b in range(B):
                own = slice(b * BLK, (b + 1) * BLK)
                dve.tensor_scalar(tile_hot[:, own, 1, :], tile_hot[:, own, 0, :], part_f[:, b:b + 1], None, ALU.mult)
                dve.tensor_tensor(tile_hot[:, own, 2, :], tile_hot[:, own, 0, :], over(iota_b[:, 0:BLK], NT), ALU.mult)
                dve.tensor_tensor(slot_hot[:, own, :], over(slot_b[:, own], P), along(iota_b[:, :], BLK),
                                  ALU.is_equal).then_inc(hots_ready, 1)

            def add_idle(q):
                dve.wait_ge(x_again[q], 16)
                tokens = acc[0][:, piece(q), :]
                dve.tensor_tensor(tokens, tokens, four(idle_row[:, :]), ALU.add).then_inc(dve_idle_added, 1)

            dve.wait_ge(found_ready, 1)
            chain(dve.tensor_copy(found[:, :, :], ps_list.rearrange("p (a k) -> p a k", k=NT)))
            dve.tensor_scalar(missing[:, :], found[:, 0, :], -float(ROWS), float(ROWS), ALU.mult, ALU.add)
            chain(dve.scalar_tensor_tensor(out=row_id[:, :], in0=found[:, 1, :], scalar=float(BLK),
                                           in1=found[:, 2, :], op0=ALU.mult, op1=ALU.add))
            dve.tensor_copy(gather_at[:, 0:NT], row_id[:, :]).then_inc(list_ready, 1)
            dve.tensor_tensor(scatter_at[:, 0:NT], missing[:, :], row_id[:, :], ALU.add).then_inc(list_ready, 1)

            add_idle(2)
            add_idle(3)

            dve.wait_ge(list_ready, 2)
            general = dve.value_load(tiles_kind[0:1, 0:1], min_val=0, max_val=NT - 1)
            singles = dve.value_load(tiles_kind[0:1, 1:2], min_val=0, max_val=NT - 1)
            dve.wait_ge(channel_ready, 2)

            def single_key(group, side):
                dve.wait_ge(single_spk_got[side % 2], group * (16 * RING // 2) + side // 2 * 16 + 16)
                dve.tensor_tensor_reduce(single_spk[side % 2], single_spk[side % 2], channel, 1.0, 0.0, ALU.mult,
                                         ALU.add, key_f[side][:, :]).then_inc(key_summed, 1)
                dve.wait_ge(key_summed, group * RING + side + 1)
                dve.tensor_scalar(key_i[side][:, :], key_f[side][:, :], 0.0, float(D - 1), ALU.max, ALU.min).then_inc(key_ready, 1)

            def single_add(group, side):
                at = group * 16 + (16 if side > 0 else 0)
                side = (side - 1) % RING
                dve.wait_ge(single_x_got[side], at)
                dve.wait_ge(table_row_got[side], at)
                dve.tensor_tensor(single_x[side], single_x[side], table_got[side], ALU.add).then_inc(single_summed, 1)

            with dve.If(singles > 0):
                with dve.Fori(0, (singles + 1 + RING - 1) // RING) as group:
                    for side in range(RING):
                        tile = group * RING + side
                        with dve.If(tile < singles):
                            single_key(group, side)
                        with dve.If(tile >= 1):
                            with dve.If(tile < singles + 1):
                                single_add(group, side)

            def add_products(tile, pair, side):
                dve.wait_ge(xrow_got[side], pair * 16 + 16)
                dve.wait_ge(out_summed, tile + 1)
                dve.tensor_tensor(x_got[side], ps_out[:, :], x_got[side], ALU.add).then_inc(row_added, 1)

            over_pairs(dve, general, add_products)

        @block.tensor
        def _(pe):
            pe.wait_ge(const_ready, 2)

            def turn_totals(b):
                pe.wait_ge(sums_ready[b], 1)
                if b > 0:
                    pe.wait_ge(before_ready, b)
                for c in range(DC):
                    last = pe.transpose(ps_turn[:, c * P:(c + 1) * P], acc[b][:, BLK - 1, c * P:(c + 1) * P], ident[:, :])
                last.then_inc(totals_turned, 1)

            def turn_before(b):
                pe.wait_ge(before_ready, b + 1)
                for c in range(DC):
                    last = pe.transpose(ps_before[:, c * P:(c + 1) * P], block_sum[:, c, 0:P], ident[:, :])
                last.then_inc(before_turned, 1)

            def turn_w1(m):
                if m == 0:
                    pe.wait_ge(idle_ready, 1)
                else:
                    pe.wait_ge(table_hidden_ready, m)
                if m % (FC // WQ) == 0:
                    pe.wait_ge(w1_in[m // (FC // WQ)], 16)
                for c in range(DC):
                    last = pe.transpose(ps_spk[:, c * P:(c + 1) * P], w1_sb[:, c, m * P:(m + 1) * P], ident[:, :])
                last.then_inc(w1_turned, 1)

            def add_b2(to):
                pe.matmul(to[:, :], ones[0:1, :], b2_row[:, :], start=True, stop=False)

            pe.wait_ge(b1_in, 16)
            pe.transpose(ps_small[:, 0:FC], b1_rows[:, :], ident[0:FC, 0:FC]).then_inc(b1_turned, 1)
            pe.wait_ge(b2_in, 16)
            add_b2(ps_idle)
            turn_totals(0)
            add_b2(ps_table[0])
            turn_before(0)
            for c in range(1, DC):
                add_b2(ps_table[c])
            pe.wait_ge(b1_ready, 2)
            for m in range(FC):
                if m % (FC // WQ) == 0:
                    pe.wait_ge(w2_in[m // (FC // WQ)], 16)
                last = pe.matmul(ps_idle[:, :], relu_b1[:, m:m + 1].to_broadcast([P, P]), w2_sb[:, m, :], start=False, stop=(m == FC - 1))
            last.then_inc(idle_summed, 1)

            turn_w1(0)
            for m in range(FC):
                if m + 1 < FC:
                    turn_w1(m + 1)
                pe.wait_ge(table_hidden_ready, m + 1)
                for c in range(DC):
                    last = pe.matmul(ps_table[c][:, :], table_hidden[m % 2][:, c, :], w2_sb[:, m, :], start=False, stop=(m == FC - 1))
                last.then_inc(table_summed, 1)
                if m == TOTALS_AT:
                    turn_totals(1)
                if m == BEFORE_AT:
                    pe.wait_ge(sum_ready, XQ)
                    turn_before(1)
                if m == LIST_AT:
                    for j in range(TOK):
                        if j % BLK == 0:
                            pe.wait_ge(hots_ready, j // BLK + 1)
                        last = pe.matmul(ps_list, slot_hot[:, j, :], tile_hot[:, j, :, :].rearrange("p a k -> p (a k)"),
                                         start=(j == 0), stop=(j == TOK - 1))
                    last.then_inc(found_ready, 1)
                if m == KINDS_AT:
                    pe.wait_ge(kinds_counted, 1)
                    pe.matmul(ps_small[:, 0:2], upper[:, :], kind_run[:, :, TOK - 1], start=True, stop=True)
                    pe.matmul(ps_small[:, 2:4], ones[:, :], kind_run[:, :, TOK - 1], start=True, stop=True).then_inc(kinds_before, 1)

            def turn_spikes(pair, side):
                pe.wait_ge(spk_got[side], pair * 16 + 16)
                for c in range(DC):
                    last = pe.transpose(ps_spk[:, c * P:(c + 1) * P], spk_rows[side][:, c * P:(c + 1) * P], ident[:, :])
                last.then_inc(spk_turned, 1)

            def ffn_tile(tile, pair, side):
                if side == 0:
                    with pe.If(pair < 1):
                        turn_spikes(0, 0)
                pe.wait_ge(spk_copied, tile + 1)
                for m in range(FC):
                    if m >= 2:
                        pe.wait_ge(hidden_ready, tile * FC + m - 1)
                    for c in range(DC):
                        last = pe.matmul(ps_hidden[m % 2][:, 0:P], w1_sb[:, c, m * P:(m + 1) * P],
                                         spk_t[:, c, :], start=(c == 0), stop=(c == DC - 1))
                    last.then_inc(hidden_summed, 1)
                with pe.If(tile + 1 < general):
                    turn_spikes(pair + side, 1 - side)
                pe.wait_ge(row_added, tile + 1)
                add_b2(ps_out)
                for m in range(FC):
                    pe.wait_ge(hidden_ready, tile * FC + m + 1)
                    last = pe.matmul(ps_out[:, :], hidden[:, m, :], w2_sb[:, m, :],
                                     start=False, stop=(m == FC - 1))
                last.then_inc(out_summed, 1)

            pe.wait_ge(list_ready, 2)
            general = pe.value_load(tiles_kind[0:1, 0:1], min_val=0, max_val=NT - 1)
            pe.wait_ge(table_rows_ready, DC)
            over_pairs(pe, general, ffn_tile)


def kernel(**inputs):
    import concourse.bacc as bacc
    from concourse.bass_utils import run_bass_kernel_spmd

    nc = bacc.Bacc("TRN2", target_bir_lowering=False, num_devices=1)
    arrays, args = {}, []
    for name in ["x", "cond_1024", "L0_ffn_w1", "L0_ffn_b1", "L0_ffn_w2", "L0_ffn_b2"]:
        a = np.ascontiguousarray(inputs[name])
        arrays[f"in_{name}"] = a
        args.append(nc.dram_tensor(f"in_{name}", a.shape, mybir.dt.from_np(a.dtype), kind="ExternalInput").ap())
    shape = inputs["x"].shape
    spikes = nc.dram_tensor("spikes", (shape[0] * shape[1], shape[2]), F32, kind="Internal").ap()
    table = nc.dram_tensor("table", (shape[2], shape[2]), F32, kind="Internal").ap()
    out = nc.dram_tensor("out", shape, F32, kind="ExternalOutput").ap()
    spike_ffn(nc, *args, spikes, table, out)
    r = run_bass_kernel_spmd(nc, [arrays], core_ids=[0])
    return r.results[0]["out"]
```
